# Optimizing a Trainium2 kernel written in Bass

```python
import numpy as np
import jax
import jax.numpy as jnp

def _softmax(x, axis=-1):
    return jax.nn.softmax(x, axis=axis)

def _gelu(x):
    return jax.nn.gelu(x, approximate=True)

def _silu(x):
    return jax.nn.silu(x)

def _sigmoid(x):
    return jax.nn.sigmoid(x)

def _layernorm(x, axis=-1, eps=1e-05):
    m = jnp.mean(x, axis=axis, keepdims=True)
    v = jnp.var(x, axis=axis, keepdims=True)
    return (x - m) / jnp.sqrt(v + eps)

def _scatter_add(tgt, idx, src, axis=0):
    return tgt.at[idx].add(src)

def _segment_sum(src, seg, n):
    return jax.ops.segment_sum(src, seg, n)
kernel_name = 'mk_prb_d1_jaxref_r8_8e272d'

def setup_inputs(seed: int=0):
    np.random.seed(seed)
    _w = jnp.asarray

    def _L0_attn_setup():
        import jax, jax.numpy as jnp
        import numpy as np
        B, N, C, H = (8, 512, 128, 16)
        D = C // H
        EPS = 1e-12

        def _l2norm(x):
            n = jnp.sqrt(jnp.sum(x * x, axis=-1, keepdims=True))
            return x / jnp.maximum(n, EPS)
        key = jax.random.key(seed)
        ks = jax.random.split(key, 5)
        return {'x': jax.random.normal(ks[0], (B, N, C), dtype=jnp.float32), 'qkv_w': jax.random.normal(ks[1], (C, 3 * C), dtype=jnp.float32) * 0.02, 'qkv_b': jax.random.normal(ks[2], (3 * C,), dtype=jnp.float32) * 0.02, 'proj_w': jax.random.normal(ks[3], (C, C), dtype=jnp.float32) * 0.02, 'proj_b': jax.random.normal(ks[4], (C,), dtype=jnp.float32) * 0.02}
    _L0_attn_in = _L0_attn_setup()

    def _L0_ffn_setup():
        import jax, jax.numpy as jnp
        import numpy as np
        B, L, D = (4, 256, 128)
        H = 16
        E = 16
        NS = 16
        S = NS // E
        F = 512
        EPS = 1e-05

        def _layernorm(x, g, b):
            mu = jnp.mean(x, axis=-1, keepdims=True)
            var = jnp.mean(jnp.square(x - mu), axis=-1, keepdims=True)
            return (x - mu) * jax.lax.rsqrt(var + EPS) * g + b

        def _mha(q, k, v, Wq, bq, Wk, bk, Wv, bv, Wo, bo):
            Bq, Lq, Dm = q.shape
            dh = Dm // H
            qh = (q @ Wq + bq).reshape(Bq, Lq, H, dh)
            kh = (k @ Wk + bk).reshape(Bq, -1, H, dh)
            vh = (v @ Wv + bv).reshape(Bq, -1, H, dh)
            scores = jnp.einsum('bqhd,bkhd->bhqk', qh, kh) / jnp.asarray(np.sqrt(dh), q.dtype)
            attn = jax.nn.softmax(scores, axis=-1)
            out = jnp.einsum('bhqk,bkhd->bqhd', attn, vh).reshape(Bq, Lq, Dm)
            return out @ Wo + bo
        key = jax.random.key(seed)
        ks = jax.random.split(key, 32)
        s = 0.02
        d = {}
        d['x'] = jax.random.normal(ks[0], (B, L, D), jnp.float32)
        d['slot_query'] = jax.random.normal(ks[1], (1, NS, D), jnp.float32) * 0.01
        for i, nm in enumerate(['d_Wq', 'd_Wk', 'd_Wv', 'd_Wo']):
            d[nm] = jax.random.normal(ks[2 + i], (D, D), jnp.float32) * s
        for nm in ['d_bq', 'd_bk', 'd_bv', 'd_bo']:
            d[nm] = jnp.zeros((D,), jnp.float32)
        for i, nm in enumerate(['c_Wq', 'c_Wk', 'c_Wv', 'c_Wo']):
            d[nm] = jax.random.normal(ks[6 + i], (D, D), jnp.float32) * s
        for nm in ['c_bq', 'c_bk', 'c_bv', 'c_bo']:
            d[nm] = jnp.zeros((D,), jnp.float32)
        d['e_ln_g'] = jnp.ones((E, D), jnp.float32)
        d['e_ln_b'] = jnp.zeros((E, D), jnp.float32)
        d['e_W1'] = jax.random.normal(ks[10], (E, D, F), jnp.float32) * s
        d['e_b1'] = jnp.zeros((E, F), jnp.float32)
        d['e_Wg'] = jax.random.normal(ks[11], (E, D, F), jnp.float32) * s
        d['e_bg'] = jnp.zeros((E, F), jnp.float32)
        d['e_W2'] = jax.random.normal(ks[12], (E, F, D), jnp.float32) * s
        d['e_b2'] = jnp.zeros((E, D), jnp.float32)
        return d
    _L0_ffn_in = _L0_ffn_setup()
    _d = {'L0_attn_x': _L0_attn_in['x'], 'L0_attn_qkv_w': _L0_attn_in['qkv_w'], 'L0_attn_qkv_b': _L0_attn_in['qkv_b'], 'L0_attn_proj_w': _L0_attn_in['proj_w'], 'L0_attn_proj_b': _L0_attn_in['proj_b'], 'L0_ffn_slot_query': _L0_ffn_in['slot_query'], 'L0_ffn_d_Wq': _L0_ffn_in['d_Wq'], 'L0_ffn_d_Wk': _L0_ffn_in['d_Wk'], 'L0_ffn_d_Wv': _L0_ffn_in['d_Wv'], 'L0_ffn_d_Wo': _L0_ffn_in['d_Wo'], 'L0_ffn_d_bq': _L0_ffn_in['d_bq'], 'L0_ffn_d_bk': _L0_ffn_in['d_bk'], 'L0_ffn_d_bv': _L0_ffn_in['d_bv'], 'L0_ffn_d_bo': _L0_ffn_in['d_bo'], 'L0_ffn_c_Wq': _L0_ffn_in['c_Wq'], 'L0_ffn_c_Wk': _L0_ffn_in['c_Wk'], 'L0_ffn_c_Wv': _L0_ffn_in['c_Wv'], 'L0_ffn_c_Wo': _L0_ffn_in['c_Wo'], 'L0_ffn_c_bq': _L0_ffn_in['c_bq'], 'L0_ffn_c_bk': _L0_ffn_in['c_bk'], 'L0_ffn_c_bv': _L0_ffn_in['c_bv'], 'L0_ffn_c_bo': _L0_ffn_in['c_bo'], 'L0_ffn_e_ln_g': _L0_ffn_in['e_ln_g'], 'L0_ffn_e_ln_b': _L0_ffn_in['e_ln_b'], 'L0_ffn_e_W1': _L0_ffn_in['e_W1'], 'L0_ffn_e_b1': _L0_ffn_in['e_b1'], 'L0_ffn_e_Wg': _L0_ffn_in['e_Wg'], 'L0_ffn_e_bg': _L0_ffn_in['e_bg'], 'L0_ffn_e_W2': _L0_ffn_in['e_W2'], 'L0_ffn_e_b2': _L0_ffn_in['e_b2']}
    _x0 = _d['L0_attn_x']
    _d['L0_attn_x'] = jax.random.normal(jax.random.fold_in(jax.random.key(seed), 1), (32, 256, 128), dtype=_x0.dtype)
    del _x0
    return _d

def reference(L0_attn_x, L0_attn_qkv_w, L0_attn_qkv_b, L0_attn_proj_w, L0_attn_proj_b, L0_ffn_slot_query, L0_ffn_d_Wq, L0_ffn_d_Wk, L0_ffn_d_Wv, L0_ffn_d_Wo, L0_ffn_d_bq, L0_ffn_d_bk, L0_ffn_d_bv, L0_ffn_d_bo, L0_ffn_c_Wq, L0_ffn_c_Wk, L0_ffn_c_Wv, L0_ffn_c_Wo, L0_ffn_c_bq, L0_ffn_c_bk, L0_ffn_c_bv, L0_ffn_c_bo, L0_ffn_e_ln_g, L0_ffn_e_ln_b, L0_ffn_e_W1, L0_ffn_e_b1, L0_ffn_e_Wg, L0_ffn_e_bg, L0_ffn_e_W2, L0_ffn_e_b2):

    def _L0_attn_ref(x, qkv_w, qkv_b, proj_w, proj_b):
        import jax, jax.numpy as jnp
        import numpy as np
        B, N, C, H = (8, 512, 128, 16)
        D = C // H
        EPS = 1e-12

        def _l2norm(x):
            n = jnp.sqrt(jnp.sum(x * x, axis=-1, keepdims=True))
            return x / jnp.maximum(n, EPS)
        b, n, c = x.shape
        qkv = (x @ qkv_w + qkv_b).reshape(b, n, 3, H, D)
        qkv = jnp.transpose(qkv, (2, 0, 3, 1, 4))
        q, k, v = (qkv[0], qkv[1], qkv[2])
        q = _l2norm(q)
        k = _l2norm(k)
        kv = jnp.einsum('bhnd,bhne->bhde', k, v)
        out = jnp.einsum('bhnd,bhde->bhne', q, kv)
        out = jnp.transpose(out, (0, 2, 1, 3)).reshape(b, n, c)
        return out @ proj_w + proj_b

    def _L0_ffn_ref(x, slot_query, d_Wq, d_Wk, d_Wv, d_Wo, d_bq, d_bk, d_bv, d_bo, c_Wq, c_Wk, c_Wv, c_Wo, c_bq, c_bk, c_bv, c_bo, e_ln_g, e_ln_b, e_W1, e_b1, e_Wg, e_bg, e_W2, e_b2):
        import jax, jax.numpy as jnp
        import numpy as np
        B, L, D = (4, 256, 128)
        H = 16
        E = 16
        NS = 16
        S = NS // E
        F = 512
        EPS = 1e-05

        def _layernorm(x, g, b):
            mu = jnp.mean(x, axis=-1, keepdims=True)
            var = jnp.mean(jnp.square(x - mu), axis=-1, keepdims=True)
            return (x - mu) * jax.lax.rsqrt(var + EPS) * g + b

        def _mha(q, k, v, Wq, bq, Wk, bk, Wv, bv, Wo, bo):
            Bq, Lq, Dm = q.shape
            dh = Dm // H
            qh = (q @ Wq + bq).reshape(Bq, Lq, H, dh)
            kh = (k @ Wk + bk).reshape(Bq, -1, H, dh)
            vh = (v @ Wv + bv).reshape(Bq, -1, H, dh)
            scores = jnp.einsum('bqhd,bkhd->bhqk', qh, kh) / jnp.asarray(np.sqrt(dh), q.dtype)
            attn = jax.nn.softmax(scores, axis=-1)
            out = jnp.einsum('bhqk,bkhd->bqhd', attn, vh).reshape(Bq, Lq, Dm)
            return out @ Wo + bo
        Bx = x.shape[0]
        q = jnp.broadcast_to(slot_query, (Bx, NS, D))
        o = q + _mha(q, x, x, d_Wq, d_bq, d_Wk, d_bk, d_Wv, d_bv, d_Wo, d_bo)
        os = o.reshape(Bx, E, S, D)
        h = _layernorm(os, e_ln_g[None, :, None, :], e_ln_b[None, :, None, :])
        u = jax.nn.silu(jnp.einsum('besd,edf->besf', h, e_W1) + e_b1[None, :, None, :])
        g = jax.nn.silu(jnp.einsum('besd,edf->besf', h, e_Wg) + e_bg[None, :, None, :])
        y = jnp.einsum('besf,efd->besd', u * g, e_W2) + e_b2[None, :, None, :]
        o = o + y.reshape(Bx, NS, D)
        out = _mha(x, o, o, c_Wq, c_bq, c_Wk, c_bk, c_Wv, c_bv, c_Wo, c_bo)
        return out
    x = L0_attn_x
    xn = _layernorm(x, axis=-1)
    x = x + _L0_attn_ref(xn, L0_attn_qkv_w, L0_attn_qkv_b, L0_attn_proj_w, L0_attn_proj_b) + _L0_ffn_ref(xn, L0_ffn_slot_query, L0_ffn_d_Wq, L0_ffn_d_Wk, L0_ffn_d_Wv, L0_ffn_d_Wo, L0_ffn_d_bq, L0_ffn_d_bk, L0_ffn_d_bv, L0_ffn_d_bo, L0_ffn_c_Wq, L0_ffn_c_Wk, L0_ffn_c_Wv, L0_ffn_c_Wo, L0_ffn_c_bq, L0_ffn_c_bk, L0_ffn_c_bv, L0_ffn_c_bo, L0_ffn_e_ln_g, L0_ffn_e_ln_b, L0_ffn_e_W1, L0_ffn_e_b1, L0_ffn_e_Wg, L0_ffn_e_bg, L0_ffn_e_W2, L0_ffn_e_b2)
    return x

_drawn_inputs = setup_inputs


def setup_inputs(seed=0):
    import zlib

    import numpy as np

    out = dict(_drawn_inputs(seed))
    spreads = {'L0_ffn_d_bq': (0.0, 0.8),
     'L0_ffn_d_bk': (0.0, 2.0),
     'L0_ffn_d_bv': (0.0, 0.8),
     'L0_ffn_d_bo': (0.0, 0.8),
     'L0_ffn_c_bq': (0.0, 0.8),
     'L0_ffn_c_bk': (0.0, 2.0),
     'L0_ffn_c_bv': (0.0, 2.0),
     'L0_ffn_c_bo': (0.0, 2.0),
     'L0_ffn_e_ln_g': (1.0, 0.6),
     'L0_ffn_e_ln_b': (0.0, 0.8),
     'L0_ffn_e_b1': (0.0, 0.8),
     'L0_ffn_e_bg': (0.0, 0.8),
     'L0_ffn_e_b2': (0.0, 0.8)}
    factors = {'L0_attn_proj_b': 70.693,
     'L0_ffn_slot_query': 8.0,
     'L0_ffn_d_Wq': 8.0,
     'L0_ffn_d_Wk': 8.0,
     'L0_ffn_d_Wv': 8.0,
     'L0_ffn_d_Wo': 8.0,
     'L0_ffn_c_Wq': 8.0,
     'L0_ffn_c_Wk': 8.0,
     'L0_ffn_c_Wv': 8.0,
     'L0_ffn_c_Wo': 3.251,
     'L0_ffn_e_W1': 8.0,
     'L0_ffn_e_Wg': 8.0,
     'L0_ffn_e_W2': 8.0,
     'L0_attn_qkv_w': 2.886,
     'L0_attn_qkv_b': 8.0,
     'L0_attn_proj_w': 2.854}
    for name, (base, spread) in spreads.items():
        noise = np.random.default_rng([zlib.crc32(name.encode()), seed]).standard_normal(out[name].shape)
        drawn = base * np.exp(spread * noise) if base else spread * noise
        out[name] = jnp.asarray(drawn.astype(out[name].dtype))
    for name, factor in factors.items():
        out[name] = (out[name] * factor).astype(out[name].dtype)
    return out
```

```python
import math
from contextlib import ExitStack

import concourse.bass as bass
from concourse import mybir

P = 128
F32 = mybir.dt.float32
ALU = mybir.AluOpType
ACT = mybir.ActivationFunctionType
AX_X = mybir.AxisListType.X

LN_EPS = 1e-5
L2_GUARD = 1e-24
LN_SHIFT = 30
DMA = 16


class Step:

    def __init__(self, base, off, inside):
        self.base, self.off, self.inside = base, off, inside

    def at(self, d):
        return Step(self.base, self.off + d, self.inside)

    @property
    def par(self):
        return self.off % 2

    def ok(self, n):
        return self.inside or 0 <= self.base + self.off < n

    def val(self, c=0):
        return self.base + (self.off + c)

    def count(self, c=0):
        return self.base + (self.off + c + 1)

    def dmas(self, c=0):
        return self.base * (DMA // 2) + ((self.off + c - self.par) // 2 + 1) * DMA


def run_steps(eng, body, first, last, lo, hi):
    for i in range(first, lo):
        body(Step(i - i % 2, i % 2, False))
    with eng.Fori(lo, hi - 1, 2) as i:
        for r in range(2):
            body(Step(i, r, True))
    for i in range(hi, last + 1):
        body(Step(i - i % 2, i % 2, False))


def linear_attention_slot_experts_kernel(nc, a, out):
    x = a["L0_attn_x"]
    NB, N, C = x.shape
    H, D = 16, 8
    E, F = a["L0_ffn_e_W1"].shape[0], a["L0_ffn_e_W1"].shape[2]
    T = N // P
    HS = H * E
    HC = HS // P
    G = 4
    NG = E // G
    FK = F // P
    SC = 1.0 / math.sqrt(D)
    RING = 3
    NR = 2 * T * H
    FOLD_DMAS, REST_DMAS = 16, 10
    PE_HEAD, PE_GROUP = 2, 4
    ACT_HEAD, ACT_GROUP = 3, 3
    DVE_HEAD, DVE_GROUP = 5, 2
    DVE_ALL = DVE_HEAD + DVE_GROUP * NG + 1
    assert C == P and T == 2 and HC == 2 and G * NB == P and H * D == C

    ctx = ExitStack()
    with ctx:
        def sb(name, shape):
            return ctx.enter_context(nc.sbuf_tensor(name, shape, F32))

        def sem(name):
            return ctx.enter_context(nc.semaphore(name))

        xnT_all = sb("xnT_all", [P, NB, N])
        qn_all = sb("qn_all", [P, NB, T, C])
        M_all = sb("M_all", [P, NB, C])
        W1 = sb("W1", [P, RING, G, F])
        Wg = sb("Wg", [P, RING, G, F])
        W2 = sb("W2", [P, RING, G, FK, C])
        slots = sb("slots", [P, E, NB])
        WB = sb("WB", [P, 5 * C])
        Wslot = sb("Wslot", [P, HS])
        dWo = sb("dWo", [P, C])
        pW = sb("pW", [P, C])
        cWk = sb("cWk", [P, C])
        cWv = sb("cWv", [P, C])
        cWo = sb("cWo", [P, C])
        outb = sb("outb", [P, C])
        cols = sb("cols", [P, 4])
        rows = sb("rows", [1, 8 * C])
        sq16 = sb("sq16", [E, C])
        b1 = sb("b1", [E, F])
        bg = sb("bg", [E, F])
        b2 = sb("b2", [E, C])
        gb16 = sb("gb16", [E, 2, C])
        gbT = sb("gbT", [P, 2, E])
        ident = sb("ident", [P, P])
        bmask = sb("bmask", [P, P])
        mask16 = sb("mask16", [P, H])
        mask4 = sb("mask4", [P, G])
        sel = sb("sel", [E, E, NB])
        neg = sb("neg", [P, P])
        pos = sb("pos", [1, P])
        one = sb("one", [1, P])
        lnshift = sb("lnshift", [P, 1])
        xin = sb("xin", [P, 2, T, C])
        xn = sb("xn", [P, 2, T, C])
        xnT = sb("xnT", [P, 2, N])
        sq = sb("sq", [P, T, 2 * C])
        vv = sb("vv", [P, 2, T, 2 * C])
        qk = sb("qk", [P, 2, T, 2 * C])
        kvm = sb("kvm", [P, 2, C])
        pr = sb("pr", [P, 2, 2 * N])
        prT = sb("prT", [P, 2, 2 * N])
        rm = sb("rm", [P, G, E])
        bnst = sb("bnst", [P, 2, T, 6])
        mv = sb("mv", [P, 2, T, 2])
        small = sb("small", [P, 2, NR + T])
        ssq = sb("ssq", [P, NR])
        lnb = sb("lnb", [P, NR + T])
        rinv = sb("rinv", [P, 2, NR + T])
        nmax = sb("nmax", [P, 2, HC])
        ssum = sb("ssum", [P, 2, HC])
        rsum = sb("rsum", [P, 2, HC])
        setup_wk, setup_wkT, setup_wq = xn[:, 0, 0, :], xn[:, 0, 1, :], xn[:, 1, 0, :]
        setup_bk, setup_sqT, setup_q = xn[:, 1, 1, :], rm[:, 0, :], rm[:, 1, :]
        setup_qblk = sq[:, 0, :]
        hT = sq[:, :, :].rearrange("p a c -> p (a c)")
        o_tm = prT[:, 0, :].rearrange("p (g c) -> p g c", g=NG)
        o2_tm = prT[:, 1, :].rearrange("p (g c) -> p g c", g=NG)
        hn = pr[:, 0, :].rearrange("p (g c) -> p g c", g=NG)
        oT = pr[:, 1, :]
        silu_u = qk[:, 0, :, :].rearrange("p t c -> p (t c)")
        silu_g = qk[:, 1, :, :].rearrange("p t c -> p (t c)")
        ug = vv[:, 0, :, :].rearrange("p t c -> p (t c)")
        ugT = vv[:, 1, :, :].rearrange("p t c -> p (t c)")
        kT = sb("kT", [P, E, NB])
        vT = sb("vT", [P, E, NB])
        xr, qns, qT = xin, xn, xnT
        cqT = sq
        kblk, vblk = qk[:, :, 0, :], qk[:, :, 1, :]
        vw = vv[:, :, 0, :].rearrange("p a (k c) -> p a k c", k=HC)
        res = vv[:, :, 1, :].rearrange("p a (t c) -> p a t c", t=T)
        top, den = ssq[:, 0:T * H], lnb[:, 0:T * H]
        rden = rinv[:, :, 0:T * H]

        def ps(name, shape):
            return ctx.enter_context(nc.psum_tensor(name, shape, F32))

        psX = ps("psX", [P, 512])
        psB = ps("psB", [P, 2, T, 512])
        psS = ps("psS", [P, 512])
        psT = ps("psT", [P, 512])
        psC = ps("psC", [P, 512])
        psU, psG = psB[:, 0, 0, :], psB[:, 0, 1, :]
        psE, psY = psB[:, 1, 0, :], psB[:, 1, 1, :]
        psV, psK = psB[:, 0, 0, :], psB[:, 0, 1, :]
        psO = psB[:, 1, :, :]

        ld_fold = sem("ld_fold")
        ld_rest = sem("ld_rest")
        ld_exp = sem("ld_exp")
        ld_exp2 = sem("ld_exp2")
        pool_const = sem("pool_const")
        dve_const = sem("dve_const")
        pe_setup = sem("pe_setup")
        dve_setup = sem("dve_setup")
        x_loaded = [sem("x_loaded0"), sem("x_loaded1")]
        bn_done = sem("bn_done")
        mv_done = sem("mv_done")
        var_ready = sem("var_ready")
        xn_ready = sem("xn_ready")
        xT_done = sem("xT_done")
        xT_ready = sem("xT_ready")
        xT_saved = [sem("xT_saved0"), sem("xT_saved1")]
        qkv_done = sem("qkv_done")
        v_ready = sem("v_ready")
        sq_ready = sem("sq_ready")
        ssum_done = sem("ssum_done")
        ss_ready = sem("ss_ready")
        ln_done = sem("ln_done")
        rinv_ready = sem("rinv_ready")
        qk_ready = sem("qk_ready")
        q_saved = [sem("q_saved0"), sem("q_saved1")]
        kv_done = sem("kv_done")
        kvm_ready = sem("kvm_ready")
        slot_done = sem("slot_done")
        slot_masked = sem("slot_masked")
        slot_ready = sem("slot_ready")
        scores_done = sem("scores_done")
        max_ready = sem("max_ready")
        exp_ready = sem("exp_ready")
        rsum_ready = sem("rsum_ready")
        p_ready = sem("p_ready")
        pT_done = sem("pT_done")
        pT_ready = sem("pT_ready")
        e_pe = sem("e_pe")
        e_act = sem("e_act")
        e_dve = sem("e_dve")
        cq_done = sem("cq_done")
        cq_ready = sem("cq_ready")
        kblk_ready = sem("kblk_ready")
        vblk_ready = sem("vblk_ready")
        s3_done = sem("s3_done")
        top_ready = sem("top_ready")
        sub_ready = sem("sub_ready")
        exp3_ready = sem("exp3_ready")
        den_ready = sem("den_ready")
        rden_ready = sem("rden_ready")
        p3_ready = sem("p3_ready")
        p3T_done = sem("p3T_done")
        p3T_ready = sem("p3T_ready")
        vw_done = sem("vw_done")
        vw_ready = sem("vw_ready")
        qn_loaded = [sem("qn_loaded0"), sem("qn_loaded1")]
        xr_loaded = [sem("xr_loaded0"), sem("xr_loaded1")]
        qT_done = sem("qT_done")
        qT_ready = sem("qT_ready")
        out_done = sem("out_done")
        res_ready = sem("res_ready")
        stored = [sem("stored0"), sem("stored1")]

        block = ctx.enter_context(nc.Block())

        def tokens(t, b):
            return t[bass.ds(b, 1), :, :].rearrange("o (p t) c -> (o p) t c", t=T)

        def expert_group(eng, g, done):
            e = slice(g * G, (g + 1) * G)
            r = g % RING
            eng.dma_start(W1[:, r, :, :], a["L0_ffn_e_W1"][e].rearrange("e c f -> c e f")).then_inc(done, DMA)
            eng.dma_start(Wg[:, r, :, :], a["L0_ffn_e_Wg"][e].rearrange("e c f -> c e f")).then_inc(done, DMA)
            for j in range(G):
                eng.dma_start(W2[:, r, j, :, :], a["L0_ffn_e_W2"][g * G + j].rearrange("(k p) c -> p k c", p=P))\
                   .then_inc(done, DMA)

        PER_GROUP = (2 + G) * DMA

        FIRST1, LAST1, LO1, HI1 = -3, NB + 1, 4, NB - 4
        FIRST3, LAST3, LO3, HI3 = -1, NB + 1, 6, NB - 2

        @block.sync
        def _(sp):
            def col(i, name):
                sp.dma_start(cols[:, i:i + 1], a[name].rearrange("(p o) -> p o", o=1)).then_inc(ld_fold, DMA)

            def row(i, name):
                n = a[name].shape[0]
                sp.dma_start(rows[:, i * C:i * C + n], a[name].rearrange("(o n) -> o n", o=1)).then_inc(ld_fold, DMA)

            sp.dma_start(WB[:, 0:3 * C], a["L0_attn_qkv_w"]).then_inc(ld_fold, DMA)
            sp.dma_start(WB[:, 3 * C:4 * C], a["L0_ffn_d_Wv"]).then_inc(ld_fold, DMA)
            sp.dma_start(WB[:, 4 * C:5 * C], a["L0_ffn_c_Wq"]).then_inc(ld_fold, DMA)
            sp.dma_start(setup_wk, a["L0_ffn_d_Wk"]).then_inc(ld_fold, DMA)
            sp.dma_start(setup_wq, a["L0_ffn_d_Wq"]).then_inc(ld_fold, DMA)
            sp.dma_start(sq16[:, :], a["L0_ffn_slot_query"][0]).then_inc(ld_fold, DMA)
            for i, name in enumerate(("L0_ffn_d_bq", "L0_ffn_d_bk", "L0_ffn_c_bk", "L0_ffn_c_bv")):
                col(i, name)
            for i, name in ((0, "L0_attn_qkv_b"), (3, "L0_ffn_d_bv"), (4, "L0_ffn_c_bq"), (5, "L0_ffn_d_bo"),
                            (6, "L0_attn_proj_b"), (7, "L0_ffn_c_bo")):
                row(i, name)

            def step(i):
                b = i.at(-2)
                if b.ok(NB):
                    sp.wait_ge(qk_ready, b.count())
                    sp.dma_start(qn_all[:, bass.ds(b.val(), 1), :, :], qk[:, b.par:b.par + 1, :, 0:C])\
                      .then_inc(q_saved[b.par], DMA)
                b = i.at(3)
                if b.ok(NB):
                    if b.inside or b.val() >= 2:
                        sp.wait_ge(xn_ready, b.count(-2))
                    sp.dma_start(xin[:, b.par, :, :], tokens(x, b.val())).then_inc(x_loaded[b.par], DMA)
                b = i.at(0)
                if b.ok(NB):
                    sp.wait_ge(xT_ready, b.count())
                    sp.dma_start(xnT_all[:, bass.ds(b.val(), 1), :], xnT[:, b.par:b.par + 1, :])\
                      .then_inc(xT_saved[b.par], DMA)

            run_steps(sp, step, FIRST1, LAST1, LO1, HI1)
            for g in range(RING, NG):
                sp.wait_ge(e_pe, PE_GROUP * (g - RING + 1) + PE_HEAD)
                expert_group(sp, g, ld_exp2)

            def step3(i):
                b = i.at(-3)
                if b.ok(NB):
                    sp.wait_ge(res_ready, b.count())
                    sp.dma_start(tokens(out, b.val()), res[:, b.par, :, :]).then_inc(stored[b.par], DMA)
                b = i.at(-1)
                if b.ok(NB):
                    if b.inside or b.val() >= 2:
                        sp.wait_ge(res_ready, b.count(-2))
                    sp.dma_start(xr[:, b.par, :, :], tokens(x, b.val())).then_inc(xr_loaded[b.par], DMA)
                b = i.at(2)
                if b.ok(NB):
                    if b.inside or b.val() >= 2:
                        sp.wait_ge(qT_done, b.count(-2))
                    sp.dma_start(qns[:, b.par:b.par + 1, :, :], qn_all[:, bass.ds(b.val(), 1), :, :])\
                      .then_inc(qn_loaded[b.par], DMA)

            for r in range(2):
                sp.wait_ge(q_saved[r], DMA * NB // 2)
            run_steps(sp, step3, -2, LAST3 + 1, LO3, HI3)
            for r in range(2):
                sp.wait_ge(stored[r], DMA * NB // 2)

        @block.gpsimd
        def _(pool):
            def select(out_, compare, base, pattern, channel):
                return pool.affine_select(out=out_, in_=out_, compare_op=compare, fill=0.0, base=base,
                                          pattern=pattern, channel_multiplier=channel)

            pool.memset(ident[:, :], 1.0)
            pool.memset(mask16[:, :], 1.0)
            pool.memset(sel[:, :, :], 1.0)
            pool.memset(neg[:, :], -1.0 / C)
            pool.memset(pos[:, :], 1.0 / C)
            pool.memset(one[:, :], 1.0)
            pool.memset(lnshift[:, :], 0.5 * LN_SHIFT * math.log(2.0)).then_inc(pool_const, 1)
            pool.wait_ge(pool_const, 1)
            select(ident[:, :], ALU.is_equal, 0, [[-1, P]], 1)
            select(sel[:, :, :], ALU.is_equal, 0, [[-1, E], [0, NB]], 1)
            select(mask16[:, :], ALU.is_ge, 0, [[-D, H]], 1).then_inc(pool_const, 1)
            pool.wait_ge(pool_const, 2)
            select(mask16[:, :], ALU.is_ge, D - 1, [[D, H]], -1).then_inc(pool_const, 1)

            def step(i):
                b = i.at(-1)
                if b.ok(NB):
                    p = b.par
                    pool.wait_ge(rsum_ready, b.count())
                    v = pr[:, p, :].rearrange("p (k n) -> p k n", k=HC)
                    pool.tensor_tensor(v, v, rsum[:, p, :].unsqueeze(2).to_broadcast([P, HC, N]), ALU.mult)\
                        .then_inc(p_ready, 1)

            run_steps(pool, step, 0, LAST1, LO1, HI1)

            heads = mask16[:, :].unsqueeze(2).to_broadcast([P, H, E])

            def step3(i):
                b = i.at(1)
                if b.ok(NB):
                    p = b.par
                    if b.inside or b.val() >= 2:
                        pool.wait_ge(s3_done, b.count(-2))
                        pool.wait_ge(vw_done, b.count(-2))
                    for blk, src, ready in ((kblk, kT, kblk_ready), (vblk, vT, vblk_ready)):
                        s = src[:, :, bass.ds(b.val(), 1)].rearrange("p e o -> p o e").to_broadcast([P, H, E])
                        pool.tensor_tensor(blk[:, p, :].rearrange("p (h e) -> p h e", h=H), s, heads, ALU.mult)\
                            .then_inc(ready, 1)
                b = i.at(0)
                if b.ok(NB):
                    p = b.par
                    pool.wait_ge(rden_ready, b.count())
                    v = pr[:, p, :].rearrange("p (h e) -> p h e", e=E)
                    pool.tensor_tensor(v, v, rden[:, p, :].unsqueeze(2).to_broadcast([P, T * H, E]), ALU.mult)\
                        .then_inc(p3_ready, 1)

            pool.wait_ge(e_dve, DVE_ALL)
            run_steps(pool, step3, FIRST3, LAST3, LO3, HI3)

        @block.scalar
        def _(act):
            def rest(dst, name):
                act.dma_start(dst, a[name]).then_inc(ld_rest, DMA)

            rest(pW[:, :], "L0_attn_proj_w")
            rest(gb16[:, 0, :], "L0_ffn_e_ln_g")
            rest(gb16[:, 1, :], "L0_ffn_e_ln_b")
            rest(dWo[:, :], "L0_ffn_d_Wo")
            rest(cWk[:, :], "L0_ffn_c_Wk")
            rest(cWv[:, :], "L0_ffn_c_Wv")
            rest(cWo[:, :], "L0_ffn_c_Wo")
            rest(b1[:, :], "L0_ffn_e_b1")
            rest(bg[:, :], "L0_ffn_e_bg")
            rest(b2[:, :], "L0_ffn_e_b2")
            act.preload_act_table_set("natural_log_exp_and_others")
            act.wait_ge(pool_const, 1)
            act.wait_ge(x_loaded[1], DMA)
            for g in range(RING):
                expert_group(act, g, ld_exp)

            def step(i):
                b = i.at(0)
                if b.ok(NB):
                    p = b.par
                    act.wait_ge(qkv_done, b.count())
                    if b.inside or b.val() >= 2:
                        act.wait_ge(slot_done, b.count(-2))
                    act.activation(vv[:, p, :, :], psB[:, p, :, 2 * C:4 * C], ACT.Copy).then_inc(v_ready, 1)
                    if b.inside or b.val() >= 1:
                        act.wait_ge(ssum_done, b.count(-1))
                    act.activation(sq[:, :, :], psB[:, p, :, 0:2 * C], ACT.Square).then_inc(sq_ready, 1)
                b = i.at(1)
                if b.ok(NB):
                    p = b.par
                    act.wait_ge(xT_done, b.count())
                    if b.inside or b.val() >= 2:
                        act.wait_ge(scores_done, b.count(-2))
                        act.wait_ge(xT_saved[p], b.dmas(-2))
                    act.activation(xnT[:, p, :], psX[:, 0:N], ACT.Copy, bias=1.0).then_inc(xT_ready, 1)
                b = i.at(-1)
                if b.ok(NB):
                    p = b.par
                    act.wait_ge(pT_done, b.count())
                    if b.inside or b.val() >= 2:
                        act.wait_ge(slot_done, b.count(-2))
                    act.activation(prT[:, p, :], psT[:, :], ACT.Copy).then_inc(pT_ready, 1)
                lo = 0 if i.ok(NB) else NR
                hi = NR + T if i.at(3).ok(NB) else NR
                if lo < hi:
                    p = i.par
                    if i.ok(NB):
                        act.wait_ge(ss_ready, i.count())
                    if i.at(3).ok(NB):
                        act.wait_ge(var_ready, i.count(3))
                    act.activation(lnb[:, lo:hi], small[:, p, lo:hi], ACT.Ln, scale=float(2 ** LN_SHIFT))\
                       .then_inc(ln_done, 1)
                    act.wait_ge(ln_done, i.count(3))
                    act.activation(rinv[:, p, lo:hi], lnb[:, lo:hi], ACT.Exp, scale=-0.5,
                                   bias=lnshift[:, 0:1]).then_inc(rinv_ready, 1)
                b = i.at(0)
                if b.ok(NB):
                    p = b.par
                    act.wait_ge(max_ready, b.count())
                    if b.inside or b.val() >= 2:
                        act.wait_ge(pT_done, b.count(-2))
                    for k in range(HC):
                        last = act.activation(pr[:, p, k * N:(k + 1) * N], psS[:, k * N:(k + 1) * N], ACT.Exp,
                                              bias=nmax[:, p, k:k + 1], accum_out=ssum[:, p, k:k + 1])
                    last.then_inc(exp_ready, 1)

            run_steps(act, step, FIRST1, LAST1, LO1, HI1)

            act.wait_ge(e_pe, 1)
            act.activation(o_tm, psE.rearrange("p (g c) -> p g c", g=NG), ACT.Copy).then_inc(e_act, 1)
            act.wait_ge(e_dve, 2)
            act.activation(lnb[:, 0:NG], small[:, 0, 0:NG], ACT.Ln).then_inc(e_act, 1)
            act.wait_ge(e_act, 2)
            act.activation(rinv[:, 0, 0:NG], lnb[:, 0:NG], ACT.Exp, scale=-0.5).then_inc(e_act, 1)
            act.preload_act_table(ACT.Silu)
            for r in range(2):
                act.wait_ge(q_saved[r], DMA * NB // 2)
            for g in range(NG):
                act.wait_ge(e_pe, PE_HEAD + PE_GROUP * g + 2)
                if g:
                    act.wait_ge(e_dve, DVE_HEAD + DVE_GROUP * (g - 1) + 1)
                act.activation(silu_u, psU, ACT.Silu).then_inc(e_act, 1)
                act.activation(silu_g, psG, ACT.Silu).then_inc(e_act, 1)
                act.wait_ge(e_pe, PE_HEAD + PE_GROUP * g + 3)
                act.activation(ugT, psT[:, :], ACT.Copy).then_inc(e_act, 1)
            act.preload_act_table_set("natural_log_exp_and_others")
            act.wait_ge(e_pe, PE_HEAD + PE_GROUP * NG + 1)
            act.activation(oT, psS[:, :], ACT.Copy).then_inc(e_act, 1)

            def step3(i):
                b = i.at(1)
                if b.ok(NB):
                    p = b.par
                    act.wait_ge(cq_done, b.count())
                    if b.inside or b.val() >= 2:
                        act.wait_ge(s3_done, b.count(-2))
                    act.activation(cqT[:, p, :], psX[:, 0:N], ACT.Copy).then_inc(cq_ready, 1)
                b = i.at(-1)
                if b.ok(NB):
                    p = b.par
                    act.wait_ge(p3T_done, b.count())
                    if b.inside or b.val() >= 2:
                        act.wait_ge(out_done, b.count(-2))
                    act.activation(prT[:, p, :], psT[:, :], ACT.Copy).then_inc(p3T_ready, 1)
                b = i.at(0)
                if b.ok(NB):
                    p = b.par
                    act.wait_ge(sub_ready, b.count())
                    act.activation(pr[:, p, :], pr[:, p, :], ACT.Exp, scale=SC).then_inc(exp3_ready, 1)
                    act.wait_ge(qT_done, b.count())
                    if b.inside or b.val() >= 2:
                        act.wait_ge(out_done, b.count(-2))
                    act.activation(qT[:, p, :], psK[:, 0:N], ACT.Copy).then_inc(qT_ready, 1)

            run_steps(act, step3, FIRST3, LAST3, LO3, HI3)

        @block.vector
        def _(dve):
            dve.wait_ge(pool_const, 3)
            dve.tensor_copy(bmask[:, :].rearrange("p (h d) -> p h d", h=H),
                            mask16[:, :].unsqueeze(2).to_broadcast([P, H, D])).then_inc(dve_const, 1)
            dve.tensor_reduce(mask4[:, :], mask16[:, :].rearrange("p (j h) -> p h j", h=G), AX_X, ALU.add)\
               .then_inc(dve_const, 1)
            dve.wait_ge(pe_setup, 1)
            dve.tensor_copy(setup_wkT, psC[:, 0:C])
            dve.tensor_copy(setup_sqT, psC[:, C:C + E])
            dve.tensor_copy(gbT[:, :, :], psC[:, C + E:C + 3 * E].rearrange("p (k e) -> p k e", k=2))
            dve.wait_ge(ld_fold, FOLD_DMAS * DMA)
            dve.memset(setup_bk, 1.0 / C).then_inc(dve_setup, 1)
            dve.wait_ge(dve_setup, 1)
            dve.tensor_scalar(setup_bk, setup_bk, cols[:, 1:2], None, ALU.mult).then_inc(dve_setup, 1)
            dve.wait_ge(pe_setup, 2)
            dve.tensor_scalar(setup_q, psX[:, 0:E], cols[:, 0:1], SC, ALU.add, ALU.mult).then_inc(dve_setup, 1)
            dve.wait_ge(dve_setup, 3)
            dve.tensor_tensor(setup_qblk.rearrange("p (h e) -> p h e", h=H),
                              setup_q.unsqueeze(1).to_broadcast([P, H, E]),
                              mask16[:, :].unsqueeze(2).to_broadcast([P, H, E]), ALU.mult).then_inc(dve_setup, 1)
            dve.wait_ge(pe_setup, 3)
            dve.tensor_tensor(WB[:, 0:4 * C], WB[:, 0:4 * C], psU, ALU.add)
            dve.tensor_tensor(WB[:, 4 * C:5 * C], WB[:, 4 * C:5 * C], psG[:, 0:C], ALU.add).then_inc(dve_setup, 1)
            dve.tensor_scalar(outb[:, :], psE[:, 0:C], 1.0 / H, None, ALU.mult).then_inc(dve_setup, 1)
            dve.wait_ge(pe_setup, 4)
            dve.tensor_copy(Wslot[:, :], psS[:, 0:HS]).then_inc(dve_setup, 1)
            dve.wait_ge(pe_setup, 5)
            dve.tensor_tensor(Wslot[:, :], Wslot[:, :], psT[:, 0:HS], ALU.add).then_inc(dve_setup, 1)

            def heads_of(t):
                return t.rearrange("p t (h d) -> p t h d", d=D)

            def step(i):
                b = i.at(-2)
                if b.ok(NB):
                    dve.wait_ge(kv_done, b.count())
                    dve.tensor_tensor(kvm[:, b.par, :], psC[:, 0:C], bmask[:, :], ALU.mult).then_inc(kvm_ready, 1)
                b = i.at(-1)
                if b.ok(NB):
                    p = b.par
                    dve.wait_ge(rinv_ready, b.count(3))
                    dve.wait_ge(v_ready, b.count())
                    if b.inside or b.val() >= 2:
                        dve.wait_ge(kv_done, b.count(-2))
                        dve.wait_ge(q_saved[p], b.dmas(-2))
                    r = rinv[:, p, 0:NR].rearrange("p (t h) -> p t h", t=T).unsqueeze(3)
                    for t in range(T):
                        last = dve.tensor_tensor(
                            qk[:, p, t, :].rearrange("p (h d) -> p h d", d=D),
                            psB[:, p, t, 0:2 * C].rearrange("p (h d) -> p h d", d=D),
                            rinv[:, p, t * 2 * H:(t + 1) * 2 * H].unsqueeze(2).to_broadcast([P, 2 * H, D]), ALU.mult)
                    last.then_inc(qk_ready, 1)
                b = i.at(-2)
                if b.ok(NB):
                    dve.wait_ge(slot_done, b.count())
                    dve.tensor_copy(M_all[:, bass.ds(b.val(), 1), :], psC[:, C:2 * C].unsqueeze(1))
                    if b.inside or b.val() >= 1:
                        dve.wait_ge(slot_ready, b.count(-1))
                    dve.tensor_tensor(rm[:, :, :], psC[:, 2 * C:2 * C + G * E].rearrange("p (h e) -> p h e", h=G),
                                      mask4[:, :].unsqueeze(2).to_broadcast([P, G, E]), ALU.mult)\
                       .then_inc(slot_masked, 1)
                b = i.at(-1)
                if b.ok(NB):
                    dve.wait_ge(exp_ready, b.count())
                    dve.reciprocal(rsum[:, b.par, :], ssum[:, b.par, :]).then_inc(rsum_ready, 1)
                b = i.at(-2)
                if b.ok(NB):
                    dve.wait_ge(slot_masked, b.count())
                    dve.tensor_reduce(slots[:, :, bass.ds(b.val(), 1)],
                                      rm[:, :, :].rearrange("p h e -> p e h"), AX_X, ALU.add).then_inc(slot_ready, 1)
                b = i.at(3)
                if b.ok(NB):
                    p = b.par
                    dve.wait_ge(x_loaded[p], b.dmas())
                    for t in range(T):
                        last = dve.bn_stats(bnst[:, p, t, :], xin[:, p, t, :])
                    last.then_inc(bn_done, 1)
                if b.ok(NB):
                    dve.wait_ge(bn_done, b.count())
                b = i.at(2)
                if b.ok(NB):
                    p = b.par
                    dve.wait_ge(rinv_ready, b.count())
                    dve.wait_ge(mv_done, b.count())
                    if b.inside or b.val() >= 2:
                        dve.wait_ge(xT_done, b.count(-2))
                    for t in range(T):
                        last = dve.tensor_scalar(xn[:, p, t, :], xin[:, p, t, :], mv[:, p, t, 0:1],
                                                 rinv[:, 1 - p, NR + t:NR + t + 1], ALU.subtract, ALU.mult)
                    last.then_inc(xn_ready, 1)
                b = i.at(3)
                if b.ok(NB):
                    p = b.par
                    for t in range(T):
                        last = dve.bn_aggr(mv[:, p, t, :], bnst[:, p, t, :])
                    last.then_inc(mv_done, 1)
                b = i.at(0)
                if b.ok(NB):
                    dve.wait_ge(scores_done, b.count())
                    dve.tensor_reduce(nmax[:, b.par, :], psS[:, :].rearrange("p (k n) -> p k n", k=HC), AX_X,
                                      ALU.max, negate=True).then_inc(max_ready, 1)
                b = i.at(3)
                if b.ok(NB):
                    dve.wait_ge(mv_done, b.count())
                    dve.tensor_scalar(small[:, i.par, NR:NR + T], mv[:, b.par, :, 1], LN_EPS, None, ALU.add)\
                       .then_inc(var_ready, 1)
                b = i.at(0)
                if b.ok(NB):
                    dve.wait_ge(sq_ready, b.count())
                    if b.inside or b.val() >= 1:
                        dve.wait_ge(ss_ready, b.count(-1))
                    dve.tensor_reduce(ssq[:, :], sq[:, :, :].rearrange("p t (h d) -> p (t h) d", d=D), AX_X,
                                      ALU.add).then_inc(ssum_done, 1)
                    dve.wait_ge(ssum_done, b.count())
                    dve.tensor_scalar(small[:, b.par, 0:NR], ssq[:, :], L2_GUARD, None, ALU.max)\
                       .then_inc(ss_ready, 1)

            run_steps(dve, step, FIRST1, LAST1, LO1, HI1)

            dve.wait_ge(e_act, 1)
            for g in range(NG):
                last = dve.bn_stats(bnst[:, g // 2, g % 2, :], o_tm[:, g, :])
            last.then_inc(bn_done, 1)
            dve.wait_ge(bn_done, NB + 1)
            for g in range(NG):
                last = dve.bn_aggr(mv[:, g // 2, g % 2, :], bnst[:, g // 2, g % 2, :])
            last.then_inc(e_dve, 1)
            dve.wait_ge(e_dve, 1)
            dve.tensor_scalar(small[:, 0, 0:NG], mv[:, :, :, 1].rearrange("p a t -> p (a t)"), LN_EPS, None, ALU.add)\
               .then_inc(e_dve, 1)
            dve.wait_ge(e_act, 3)
            for g in range(NG):
                last = dve.tensor_scalar(hn[:, g, :], o_tm[:, g, :], mv[:, g // 2, g % 2, 0:1], rinv[:, 0, g:g + 1],
                                         ALU.subtract, ALU.mult)
            last.then_inc(e_dve, 1)
            dve.wait_ge(e_pe, 2)
            h3 = hT.rearrange("p (e b) -> p e b", e=E)
            dve.tensor_tensor(h3, psX[:, :].rearrange("p (e b) -> p e b", e=E),
                              gbT[:, 0, :].unsqueeze(2).to_broadcast([P, E, NB]), ALU.mult).then_inc(e_dve, 1)
            dve.wait_ge(e_dve, 4)
            dve.tensor_tensor(h3, h3, gbT[:, 1, :].unsqueeze(2).to_broadcast([P, E, NB]), ALU.add).then_inc(e_dve, 1)
            for g in range(NG):
                dve.wait_ge(e_act, ACT_HEAD + ACT_GROUP * g + 2)
                if g:
                    dve.wait_ge(e_pe, PE_HEAD + PE_GROUP * (g - 1) + 3)
                dve.tensor_tensor(ug, silu_u, silu_g, ALU.mult).then_inc(e_dve, 1)
                dve.wait_ge(e_pe, PE_HEAD + PE_GROUP * g + 4)
                dve.tensor_tensor(o2_tm[:, g, :], psY[:, 0:C], o_tm[:, g, :], ALU.add).then_inc(e_dve, 1)
            dve.wait_ge(e_pe, PE_HEAD + PE_GROUP * NG + 2)
            dve.tensor_scalar(kT[:, :, :].rearrange("p e b -> p (e b)"), psU, cols[:, 2:3], None, ALU.add)
            dve.tensor_scalar(vT[:, :, :].rearrange("p e b -> p (e b)"), psG, cols[:, 3:4], None, ALU.add)\
               .then_inc(e_dve, 1)

            def step3(i):
                b = i.at(0)
                if b.ok(NB):
                    p = b.par
                    s3 = psS[:, :].rearrange("p (h e) -> p h e", e=E)
                    dve.wait_ge(s3_done, b.count())
                    dve.tensor_reduce(top, s3, AX_X, ALU.max).then_inc(top_ready, 1)
                    dve.wait_ge(top_ready, b.count())
                    if b.inside or b.val() >= 2:
                        dve.wait_ge(p3T_done, b.count(-2))
                    dve.tensor_tensor(pr[:, p, :].rearrange("p (h e) -> p h e", e=E), s3,
                                      top.unsqueeze(2).to_broadcast([P, T * H, E]), ALU.subtract)\
                       .then_inc(sub_ready, 1)
                b = i.at(-3)
                if b.ok(NB):
                    p = b.par
                    dve.wait_ge(out_done, b.count())
                    dve.wait_ge(xr_loaded[p], b.dmas())
                    if b.inside or b.val() >= 2:
                        dve.wait_ge(stored[p], b.dmas(-2))
                    dve.tensor_tensor(res[:, p, :, :], psO[:, p, 0:N].rearrange("p (t c) -> p t c", t=T),
                                      xr[:, p, :, :], ALU.add).then_inc(res_ready, 1)
                b = i.at(0)
                if b.ok(NB):
                    p = b.par
                    dve.wait_ge(vw_done, b.count())
                    if b.inside or b.val() >= 2:
                        dve.wait_ge(out_done, b.count(-2))
                    dve.tensor_tensor(vw[:, p, :, :], psV[:, 0:N].rearrange("p (k c) -> p k c", k=HC),
                                      outb[:, :].unsqueeze(1).to_broadcast([P, HC, C]), ALU.add).then_inc(vw_ready, 1)
                    dve.wait_ge(exp3_ready, b.count())
                    if b.inside or b.val() >= 1:
                        dve.wait_ge(rden_ready, b.count(-1))
                    dve.tensor_reduce(den, pr[:, p, :].rearrange("p (h e) -> p h e", e=E), AX_X, ALU.add)\
                       .then_inc(den_ready, 1)
                    dve.wait_ge(den_ready, b.count())
                    dve.reciprocal(rden[:, p, :], den).then_inc(rden_ready, 1)

            run_steps(dve, step3, 0, LAST3 + 1, LO3, HI3)

        @block.tensor
        def _(pe):
            pe.wait_ge(ld_fold, FOLD_DMAS * DMA)
            pe.wait_ge(ld_rest, REST_DMAS * DMA)
            pe.wait_ge(pool_const, 3)
            pe.transpose(psC[:, 0:C], setup_wk, ident[:, :])
            pe.transpose(psC[:, C:C + E], sq16[:, :], ident[0:E, 0:E])
            for k in range(2):
                last = pe.transpose(psC[:, C + (k + 1) * E:C + (k + 2) * E], gb16[:, k, :], ident[0:E, 0:E])
            last.then_inc(pe_setup, 1)
            for dst, lo, hi in ((psU, 0, 4 * C), (psG[:, 0:C], 4 * C, 5 * C)):
                pe.matmul(dst, neg[:, :], WB[:, lo:hi], start=True, stop=False)
                pe.matmul(dst, pos[:, :], rows[:, lo:hi], start=False, stop=True)
            pe.wait_ge(dve_setup, 1)
            pe.matmul(psX[:, 0:E], setup_wq, setup_sqT, start=True, stop=True).then_inc(pe_setup, 1)
            for k in range(2):
                last = pe.matmul(psE[:, 0:C], one[:, :], rows[:, (6 + k) * C:(7 + k) * C], start=(k == 0), stop=(k == 1))
            last.then_inc(pe_setup, 1)
            pe.wait_ge(dve_setup, 4)
            pe.matmul(psS[:, 0:HS], setup_wkT, setup_qblk, start=True, stop=True).then_inc(pe_setup, 1)
            pe.wait_ge(dve_setup, 7)
            pe.matmul(psT[:, 0:HS], neg[:, :], Wslot[:, :], start=True, stop=False)
            pe.matmul(psT[:, 0:HS], setup_bk, setup_qblk, start=False, stop=True).then_inc(pe_setup, 1)
            pe.wait_ge(dve_setup, 8)

            def step(i):
                def project(t):
                    b = i.at(0)
                    p = b.par
                    if t == 0:
                        pe.wait_ge(xT_ready, b.count())
                        if b.inside or b.val() >= 2:
                            pe.wait_ge(qk_ready, b.count(-2))
                    return pe.matmul(psB[:, p, t, :], xnT[:, p, t * P:(t + 1) * P], WB[:, 0:4 * C],
                                     start=True, stop=True)

                if i.ok(NB):
                    project(0)
                b = i.at(-2)
                if b.ok(NB):
                    p = b.par
                    pe.wait_ge(kvm_ready, b.count())
                    pe.matmul(psC[:, C:2 * C], kvm[:, p, :], pW[:, :], start=True, stop=True)
                    pe.wait_ge(pT_ready, b.count())
                    for j in range(4):
                        for t in range(T):
                            last = pe.matmul(psC[32 * j:32 * j + 32, 2 * C:2 * C + G * E],
                                             vv[:, p, t, C + 32 * j:C + 32 * j + 32],
                                             prT[:, p, t * HS + j * G * E:t * HS + (j + 1) * G * E],
                                             start=(t == 0), stop=(t == T - 1))
                    last.then_inc(slot_done, 1)
                if i.ok(NB):
                    project(1).then_inc(qkv_done, 1)
                b = i.at(1)
                if b.ok(NB):
                    p = b.par
                    pe.wait_ge(xn_ready, b.count())
                    if b.inside or b.val() >= 1:
                        pe.wait_ge(xT_ready, b.count(-1))
                    for t in range(T):
                        last = pe.transpose(psX[:, t * P:(t + 1) * P], xn[:, p, t, :], ident[:, :])
                    last.then_inc(xT_done, 1)
                b = i.at(0)
                if b.ok(NB):
                    if b.inside or b.val() >= 1:
                        pe.wait_ge(exp_ready, b.count(-1))
                    for k in range(HC):
                        last = pe.matmul(psS[:, k * N:(k + 1) * N], Wslot[:, k * P:(k + 1) * P], xnT[:, b.par, :],
                                         start=True, stop=True)
                    last.then_inc(scores_done, 1)
                b = i.at(-1)
                if b.ok(NB):
                    p = b.par
                    pe.wait_ge(p_ready, b.count())
                    if b.inside or b.val() >= 1:
                        pe.wait_ge(pT_ready, b.count(-1))
                    for t in range(T):
                        for k in range(HC):
                            last = pe.transpose(psT[:, t * HS + k * P:t * HS + (k + 1) * P],
                                                pr[:, p, k * N + t * P:k * N + (t + 1) * P], ident[:, :])
                    last.then_inc(pT_done, 1)
                    pe.wait_ge(qk_ready, b.count())
                    if b.inside or b.val() >= 1:
                        pe.wait_ge(slot_masked, b.count(-1))
                    for t in range(T):
                        last = pe.matmul(psC[:, 0:C], vv[:, p, t, 0:C], qk[:, p, t, C:2 * C],
                                         start=(t == 0), stop=(t == T - 1))
                    last.then_inc(kv_done, 1)

            run_steps(pe, step, -1, LAST1, LO1, HI1)

            pe.wait_ge(slot_ready, NB)
            for g in range(NG):
                cols_g = slice(g * G, (g + 1) * G)
                pe.matmul(psE[:, g * C:(g + 1) * C], slots[:, cols_g, :].rearrange("p e b -> p (e b)"), dWo[:, :],
                          start=True, stop=False)
                pe.matmul(psE[:, g * C:(g + 1) * C], sel[:, cols_g, :].rearrange("p e b -> p (e b)"), sq16[:, :],
                          start=False, stop=False)
                last = pe.matmul(psE[:, g * C:(g + 1) * C], one[:, :], rows[:, 5 * C:6 * C], start=False, stop=True)
            last.then_inc(e_pe, 1)
            pe.wait_ge(e_dve, 3)
            for g in range(NG):
                last = pe.transpose(psX[:, g * C:(g + 1) * C], hn[:, g, :], ident[:, :])
            last.then_inc(e_pe, 1)
            pe.wait_ge(e_dve, 5)
            pe.wait_ge(ld_exp, RING * PER_GROUP)

            def up(g):
                if g >= RING:
                    pe.wait_ge(ld_exp2, (g - RING + 1) * PER_GROUP)
                if g:
                    pe.wait_ge(e_act, ACT_HEAD + ACT_GROUP * (g - 1) + 2)
                for dst, w, bias in ((psU, W1, b1), (psG, Wg, bg)):
                    pe.matmul(dst, sel[:, g * G:(g + 1) * G, :].rearrange("p e b -> p (e b)"), bias[:, :],
                              start=True, stop=False, skip_group_check=True)
                    for j in range(G):
                        e = g * G + j
                        last = pe.matmul(dst[NB * j:NB * (j + 1), :], hT[:, e * NB:(e + 1) * NB],
                                         w[:, g % RING, j, :], start=False, stop=True, skip_group_check=True)
                    last.then_inc(e_pe, 1)

            for g in range(NG):
                up(g)
                pe.wait_ge(e_dve, DVE_HEAD + DVE_GROUP * g + 1)
                if g:
                    pe.wait_ge(e_act, ACT_HEAD + ACT_GROUP * (g - 1) + 3)
                for k in range(FK):
                    last = pe.transpose(psT[:, k * P:(k + 1) * P], ug[:, k * P:(k + 1) * P], ident[:, :])
                last.then_inc(e_pe, 1)
                pe.wait_ge(e_act, ACT_HEAD + ACT_GROUP * g + 3)
                if g:
                    pe.wait_ge(e_dve, DVE_HEAD + DVE_GROUP * (g - 1) + 2)
                pe.matmul(psY[:, 0:C], sel[:, g * G:(g + 1) * G, :].rearrange("p e b -> p (e b)"), b2[:, :],
                          start=True, stop=False, skip_group_check=True)
                for k in range(FK):
                    for j in range(G):
                        last = pe.matmul(psY[NB * j:NB * (j + 1), 0:C], ugT[:, k * P + NB * j:k * P + NB * (j + 1)],
                                         W2[:, g % RING, j, k, :], start=False, stop=(k == FK - 1),
                                         skip_group_check=True)
                last.then_inc(e_pe, 1)
            pe.wait_ge(e_dve, DVE_HEAD + DVE_GROUP * NG)
            for g in range(NG):
                last = pe.transpose(psS[:, g * C:(g + 1) * C], o2_tm[:, g, :], ident[:, :])
            last.then_inc(e_pe, 1)
            pe.wait_ge(e_act, ACT_HEAD + ACT_GROUP * NG + 1)
            pe.matmul(psU, cWk[:, :], oT, start=True, stop=True)
            pe.matmul(psG, cWv[:, :], oT, start=True, stop=True).then_inc(e_pe, 1)

            for r in range(2):
                pe.wait_ge(xT_saved[r], DMA * NB // 2)
            pe.wait_ge(e_dve, DVE_ALL)

            def step3(i):
                b = i.at(0)
                if b.ok(NB):
                    p = b.par
                    pe.wait_ge(cq_ready, b.count())
                    pe.wait_ge(kblk_ready, b.count())
                    if b.inside or b.val() >= 1:
                        pe.wait_ge(sub_ready, b.count(-1))
                    for t in range(T):
                        last = pe.matmul(psS[:, t * HS:(t + 1) * HS], cqT[:, p, t * P:(t + 1) * P], kblk[:, p, :],
                                         start=True, stop=True)
                    last.then_inc(s3_done, 1)
                b = i.at(1)
                if b.ok(NB):
                    if b.inside or b.val() >= 1:
                        pe.wait_ge(cq_ready, b.count(-1))
                    pe.matmul(psX[:, 0:N], WB[:, 4 * C:5 * C],
                              xnT_all[:, bass.ds(b.val(), 1), :].rearrange("p o n -> p (o n)"),
                              start=True, stop=True).then_inc(cq_done, 1)
                b = i.at(0)
                if b.ok(NB):
                    p = b.par
                    pe.wait_ge(vblk_ready, b.count())
                    if b.inside or b.val() >= 1:
                        pe.wait_ge(vw_ready, b.count(-1))
                    for k in range(HC):
                        last = pe.matmul(psV[:, k * C:(k + 1) * C], vblk[:, p, k * P:(k + 1) * P], cWo[:, :],
                                         start=True, stop=True)
                    last.then_inc(vw_done, 1)
                b = i.at(-1)
                if b.ok(NB):
                    p = b.par
                    pe.wait_ge(p3_ready, b.count())
                    if b.inside or b.val() >= 1:
                        pe.wait_ge(p3T_ready, b.count(-1))
                    for k in range(HC):
                        for t in range(T):
                            last = pe.transpose(psT[:, k * N + t * P:k * N + (t + 1) * P],
                                                pr[:, p, t * HS + k * P:t * HS + (k + 1) * P], ident[:, :])
                    last.then_inc(p3T_done, 1)
                b = i.at(0)
                if b.ok(NB):
                    p = b.par
                    pe.wait_ge(qn_loaded[p], b.dmas())
                    if b.inside or b.val() >= 1:
                        pe.wait_ge(qT_ready, b.count(-1))
                    for t in range(T):
                        last = pe.transpose(psK[:, t * P:(t + 1) * P], qns[:, p, t, :], ident[:, :])
                    last.then_inc(qT_done, 1)
                b = i.at(-2)
                if b.ok(NB):
                    p = b.par
                    pe.wait_ge(p3T_ready, b.count())
                    pe.wait_ge(vw_ready, b.count())
                    pe.wait_ge(qT_ready, b.count())
                    if b.inside or b.val() >= 2:
                        pe.wait_ge(res_ready, b.count(-2))
                    for t in range(T):
                        dst = psO[:, p, t * C:(t + 1) * C]
                        pe.matmul(dst, qT[:, p, t * P:(t + 1) * P],
                                  M_all[:, bass.ds(b.val(), 1), :].rearrange("p o c -> p (o c)"),
                                  start=True, stop=False)
                        for k in range(HC):
                            last = pe.matmul(dst, prT[:, p, k * N + t * P:k * N + (t + 1) * P], vw[:, p, k, :],
                                             start=False, stop=(k == HC - 1))
                    last.then_inc(out_done, 1)

            run_steps(pe, step3, FIRST3, LAST3, LO3, HI3)


def kernel(**inputs):
    import numpy as _np
    import concourse.bacc as _bacc
    from concourse import mybir as _mybir
    from concourse.bass_utils import run_bass_kernel_spmd as _run

    nc = _bacc.Bacc("TRN2", target_bir_lowering=False, num_devices=1)
    arrays, aps = {}, {}
    for name, value in inputs.items():
        v = _np.ascontiguousarray(value)
        arrays[f"in_{name}"] = v
        aps[name] = nc.dram_tensor(f"in_{name}", v.shape, _mybir.dt.from_np(v.dtype), kind="ExternalInput").ap()
    shape = inputs["L0_attn_x"].shape
    out = nc.dram_tensor("out", shape, _mybir.dt.float32, kind="ExternalOutput").ap()
    linear_attention_slot_experts_kernel(nc, aps, out)
    r = _run(nc, [arrays], core_ids=[0])
    return r.results[0]["out"]
```

```python
import math
from contextlib import ExitStack

import concourse.bass as bass
from concourse import mybir

P = 128
F32 = mybir.dt.float32
BF16 = mybir.dt.bfloat16
ALU = mybir.AluOpType
ACT = mybir.ActivationFunctionType
AX_X = mybir.AxisListType.X

LN_EPS = 1e-5
L2_GUARD = 1e-24
LN_SHIFT = 30
DMA = 16


class Step:

    def __init__(self, base, off, inside):
        self.base, self.off, self.inside = base, off, inside

    def at(self, d):
        return Step(self.base, self.off + d, self.inside)

    @property
    def par(self):
        return self.off % 2

    def ok(self, n):
        return self.inside or 0 <= self.base + self.off < n

    def val(self, c=0):
        return self.base + (self.off + c)

    def count(self, c=0):
        return self.base + (self.off + c + 1)

    def dmas(self, c=0):
        return self.base * (DMA // 2) + ((self.off + c - self.par) // 2 + 1) * DMA


def run_steps(eng, body, first, last, lo, hi):
    for i in range(first, lo):
        body(Step(i - i % 2, i % 2, False))
    with eng.Fori(lo, hi - 1, 2) as i:
        for r in range(2):
            body(Step(i, r, True))
    for i in range(hi, last + 1):
        body(Step(i - i % 2, i % 2, False))


def linear_attention_slot_experts_kernel(nc, a, out):
    x = a["L0_attn_x"]
    NB, N, C = x.shape
    H, D = 16, 8
    E, F = a["L0_ffn_e_W1"].shape[0], a["L0_ffn_e_W1"].shape[2]
    T = N // P
    HS = H * E
    HC = HS // P
    G = 4
    NG = E // G
    FK = F // P
    SC = 1.0 / math.sqrt(D)
    K3 = 64 + E
    RING = 3
    NR = 2 * T * H
    FOLD_DMAS, REST_DMAS, BIAS_DMAS = 15, 7, 5
    assert C == P and T == 2 and HC == 2 and G * NB == P and H * D == C

    ctx = ExitStack()
    with ctx:
        def sb(name, shape, dtype=F32):
            return ctx.enter_context(nc.sbuf_tensor(name, shape, dtype))

        def sem(name):
            return ctx.enter_context(nc.semaphore(name))

        xnT_all = sb("xnT_all", [P, NB, N])
        qn_all = sb("qn_all", [P, NB, T, C])
        M_all = sb("M_all", [P, NB, C])
        W1 = sb("W1", [P, RING, G, F])
        Wg = sb("Wg", [P, RING, G, F])
        W2 = sb("W2", [P, RING, G, FK, C])
        slots = sb("slots", [P, E, NB])
        WB = sb("WB", [P, 5 * C])
        Wslot = sb("Wslot", [P, HS])
        dWo = sb("dWo", [P, C])
        pW = sb("pW", [P, C])
        cWk = sb("cWk", [P, C])
        cWv = sb("cWv", [P, C])
        cWo = sb("cWo", [P, C])
        outb = sb("outb", [P, C])
        cols = sb("cols", [P, 4])
        rows = sb("rows", [1, 8 * C])
        sq16 = sb("sq16", [E, C])
        bias3 = sb("bias3", [K3, 2 * F + 2 * C], BF16)
        gb16 = sb("gb16", [E, 2, C])
        gbT = sb("gbT", [P, 2, E])
        ident = sb("ident", [P, P])
        bmask = sb("bmask", [P, P])
        mask16 = sb("mask16", [P, H])
        mask4 = sb("mask4", [P, G])
        sel = sb("sel", [K3, E, NB], BF16)
        neg = sb("neg", [P, P])
        pos = sb("pos", [1, P])
        one = sb("one", [1, P])
        lnshift = sb("lnshift", [P, 1])
        xin = sb("xin", [P, 2, T, C])
        xn = sb("xn", [P, 2, T, C])
        xnT = sb("xnT", [P, 2, N])
        sq = sb("sq", [P, T, 2 * C])
        vv = sb("vv", [P, 2, T, 2 * C])
        qk = sb("qk", [P, 2, T, 2 * C])
        kvm = sb("kvm", [P, 2, C])
        pr = sb("pr", [P, 2, 2 * N])
        prT = sb("prT", [P, 2, 2 * N])
        rm = sb("rm", [P, G, E])
        bnst = sb("bnst", [P, 2, T, 6])
        mv = sb("mv", [P, 2, T, 2])
        small = sb("small", [P, 2, NR + T])
        ssq = sb("ssq", [P, NR])
        lnb = sb("lnb", [P, NR + T])
        rinv0 = sb("rinv0", [P, 2, NR + T])
        nwt = sb("nwt", [P, 2, NR + T])
        rinv = sb("rinv", [P, 2, NR + T])
        nmax = sb("nmax", [P, 2, HC])
        ssum = sb("ssum", [P, 2, HC])
        rsum = sb("rsum", [P, 2, HC])
        setup_wk, setup_wkT, setup_wq = xn[:, 0, 0, :], xn[:, 0, 1, :], xn[:, 1, 0, :]
        setup_bk, setup_sqT, setup_q = xn[:, 1, 1, :], rm[:, 0, :], rm[:, 1, :]
        setup_qblk = sq[:, 0, :]
        bsrc = qn_all[0:E, 20:25, :, :].rearrange("p b t c -> p (b t c)")
        bmid = qn_all[0:E, 25:28, :, :].rearrange("p b t c -> p (b t c)").bitcast(BF16)[:, 0:2 * F + 2 * C]
        dbo16 = qn_all[0:E, 28, 0, :]
        hT = sq[:, :, :].rearrange("p a c -> p (a c)")
        o_tm = prT[:, 0, :].rearrange("p (g c) -> p g c", g=NG)
        o2_tm = prT[:, 1, :].rearrange("p (g c) -> p g c", g=NG)
        hn = pr[:, 0, :].rearrange("p (g c) -> p g c", g=NG)
        oT = pr[:, 1, :]
        silu_u = qk[:, 0, :, :].rearrange("p t c -> p (t c)")
        silu_g = qk[:, 1, :, :].rearrange("p t c -> p (t c)")
        ug = vv[:, 0, :, :].rearrange("p t c -> p (t c)")
        ugT = vv[:, 1, :, :].rearrange("p t c -> p (t c)")
        kT = sb("kT", [P, E, NB])
        vT = sb("vT", [P, E, NB])
        xr, qns, qT = xin, xn, xnT
        cqT = sq
        kblk, vblk = qk[:, :, 0, :], qk[:, :, 1, :]
        vw = vv[:, :, 0, :].rearrange("p a (k c) -> p a k c", k=HC)
        res = vv[:, :, 1, :].rearrange("p a (t c) -> p a t c", t=T)
        top, den = ssq[:, 0:T * H], lnb[:, 0:T * H]
        rden = rinv[:, :, 0:T * H]

        def ps(name, shape):
            return ctx.enter_context(nc.psum_tensor(name, shape, F32))

        psX = ps("psX", [P, 512])
        psB = ps("psB", [P, 2, T, 512])
        psS = ps("psS", [P, 512])
        psT = ps("psT", [P, 512])
        psC = ps("psC", [P, 512])
        psU, psG = psB[:, :, 0, :], psB[:, :, 1, :]
        psE, psY = psS[:, :], psC[:, :]
        psV, psK = psB[:, 0, 0, :], psB[:, 0, 1, :]
        psO = psB[:, 1, :, :]

        ld_fold = sem("ld_fold")
        ld_rest = sem("ld_rest")
        ld_exp = sem("ld_exp")
        ld_exp2 = sem("ld_exp2")
        ld_bias = sem("ld_bias")
        split_pool = sem("split_pool")
        split_act = sem("split_act")
        pool_const = sem("pool_const")
        ident_const = sem("ident_const")
        sel_const = sem("sel_const")
        dve_const = sem("dve_const")
        pe_setup = sem("pe_setup")
        dve_setup = sem("dve_setup")
        x_loaded = [sem("x_loaded0"), sem("x_loaded1")]
        bn_done = sem("bn_done")
        mv_done = sem("mv_done")
        var_ready = sem("var_ready")
        xm_ready = sem("xm_ready")
        xn_ready = sem("xn_ready")
        m_done = sem("m_done")
        m_ready = sem("m_ready")
        xT_done = sem("xT_done")
        xT_ready = sem("xT_ready")
        xT_saved = [sem("xT_saved0"), sem("xT_saved1")]
        qkv_done = sem("qkv_done")
        v_ready = sem("v_ready")
        sq_ready = sem("sq_ready")
        ssum_done = sem("ssum_done")
        ss_ready = sem("ss_ready")
        ln_done = sem("ln_done")
        rinv0_ready = sem("rinv0_ready")
        newton1 = sem("newton1")
        newton2 = sem("newton2")
        rinv_ready = sem("rinv_ready")
        qk_ready = sem("qk_ready")
        q_saved = [sem("q_saved0"), sem("q_saved1")]
        kv_done = sem("kv_done")
        kvm_ready = sem("kvm_ready")
        slot_done = sem("slot_done")
        slot_masked = sem("slot_masked")
        slot_ready = sem("slot_ready")
        scores_done = sem("scores_done")
        max_ready = sem("max_ready")
        exp_ready = sem("exp_ready")
        rsum_ready = sem("rsum_ready")
        p_ready = sem("p_ready")
        pT_done = sem("pT_done")
        pT_ready = sem("pT_ready")
        e_o = sem("e_o")
        e_o_ready = sem("e_o_ready")
        e_var_ready = sem("e_var_ready")
        e_ln_done = sem("e_ln_done")
        e_rinv0_ready = sem("e_rinv0_ready")
        e_newton = sem("e_newton")
        e_hn_ready = sem("e_hn_ready")
        e_hnT_done = sem("e_hnT_done")
        e_hg_done = sem("e_hg_done")
        e_h_ready = sem("e_h_ready")
        e_u_done = sem("e_u_done")
        e_g_done = sem("e_g_done")
        e_silu_ready = sem("e_silu_ready")
        e_ug_ready = sem("e_ug_ready")
        e_ugT_done = sem("e_ugT_done")
        e_ugT_ready = sem("e_ugT_ready")
        e_y_done = sem("e_y_done")
        e_o2_ready = sem("e_o2_ready")
        e_oT_done = sem("e_oT_done")
        e_oT_ready = sem("e_oT_ready")
        e_kv_done = sem("e_kv_done")
        e_kv_ready = sem("e_kv_ready")
        cq_done = sem("cq_done")
        cq_ready = sem("cq_ready")
        kblk_ready = sem("kblk_ready")
        vblk_ready = sem("vblk_ready")
        s3_done = sem("s3_done")
        top_ready = sem("top_ready")
        sub_ready = sem("sub_ready")
        exp3_ready = sem("exp3_ready")
        den_ready = sem("den_ready")
        rden_ready = sem("rden_ready")
        p3_ready = sem("p3_ready")
        p3T_done = sem("p3T_done")
        p3T_ready = sem("p3T_ready")
        vw_done = sem("vw_done")
        vw_ready = sem("vw_ready")
        qn_loaded = [sem("qn_loaded0"), sem("qn_loaded1")]
        xr_loaded = [sem("xr_loaded0"), sem("xr_loaded1")]
        qT_done = sem("qT_done")
        qT_ready = sem("qT_ready")
        out_done = sem("out_done")
        res_ready = sem("res_ready")
        stored = [sem("stored0"), sem("stored1")]

        block = ctx.enter_context(nc.Block())

        def tokens(t, b):
            return t[bass.ds(b, 1), :, :].rearrange("o (p t) c -> (o p) t c", t=T)

        def expert_group(eng, g, done):
            e = slice(g * G, (g + 1) * G)
            r = g % RING
            eng.dma_start(W1[:, r, :, :], a["L0_ffn_e_W1"][e].rearrange("e c f -> c e f")).then_inc(done, DMA)
            eng.dma_start(Wg[:, r, :, :], a["L0_ffn_e_Wg"][e].rearrange("e c f -> c e f")).then_inc(done, DMA)
            for j in range(G):
                eng.dma_start(W2[:, r, j, :, :], a["L0_ffn_e_W2"][g * G + j].rearrange("(k p) c -> p k c", p=P))\
                   .then_inc(done, DMA)

        PER_GROUP = (2 + G) * DMA

        FIRST1, LAST1, LO1, HI1 = -3, NB + 1, 4, NB - 4
        FIRST3, LAST3, LO3, HI3 = -1, NB + 1, 6, NB - 2

        @block.sync
        def _(sp):
            def col(i, name):
                sp.dma_start(cols[:, i:i + 1], a[name].rearrange("(p o) -> p o", o=1)).then_inc(ld_fold, DMA)

            def row(i, name):
                n = a[name].shape[0]
                sp.dma_start(rows[:, i * C:i * C + n], a[name].rearrange("(o n) -> o n", o=1)).then_inc(ld_fold, DMA)

            sp.dma_start(WB[:, 0:3 * C], a["L0_attn_qkv_w"]).then_inc(ld_fold, DMA)
            sp.dma_start(WB[:, 3 * C:4 * C], a["L0_ffn_d_Wv"]).then_inc(ld_fold, DMA)
            sp.dma_start(WB[:, 4 * C:5 * C], a["L0_ffn_c_Wq"]).then_inc(ld_fold, DMA)
            sp.dma_start(setup_wk, a["L0_ffn_d_Wk"]).then_inc(ld_fold, DMA)
            sp.dma_start(setup_wq, a["L0_ffn_d_Wq"]).then_inc(ld_fold, DMA)
            sp.dma_start(sq16[:, :], a["L0_ffn_slot_query"][0]).then_inc(ld_fold, DMA)
            for i, name in enumerate(("L0_ffn_d_bq", "L0_ffn_d_bk", "L0_ffn_c_bk", "L0_ffn_c_bv")):
                col(i, name)
            for i, name in ((0, "L0_attn_qkv_b"), (3, "L0_ffn_d_bv"), (4, "L0_ffn_c_bq"), (6, "L0_attn_proj_b"), (7, "L0_ffn_c_bo")):
                row(i, name)

            def step(i):
                b = i.at(-1)
                if b.ok(NB):
                    sp.wait_ge(qk_ready, b.count())
                    sp.dma_start(qn_all[:, bass.ds(b.val(), 1), :, :], qk[:, b.par:b.par + 1, :, 0:C])\
                      .then_inc(q_saved[b.par], DMA)
                b = i.at(4)
                if b.ok(NB):
                    if b.inside or b.val() >= 2:
                        sp.wait_ge(xm_ready, b.count(-2))
                    sp.dma_start(xin[:, b.par, :, :], tokens(x, b.val())).then_inc(x_loaded[b.par], DMA)
                b = i.at(1)
                if b.ok(NB):
                    sp.wait_ge(xT_ready, b.count())
                    sp.dma_start(xnT_all[:, bass.ds(b.val(), 1), :], xnT[:, b.par:b.par + 1, :])\
                      .then_inc(xT_saved[b.par], DMA)

            run_steps(sp, step, FIRST1 - 1, LAST1, LO1, HI1)
            for g in range(RING, NG):
                sp.wait_ge(e_y_done, g - RING + 1)
                expert_group(sp, g, ld_exp2)

            def step3(i):
                b = i.at(-3)
                if b.ok(NB):
                    sp.wait_ge(res_ready, b.count())
                    sp.dma_start(tokens(out, b.val()), res[:, b.par, :, :]).then_inc(stored[b.par], DMA)
                b = i.at(-1)
                if b.ok(NB):
                    if b.inside or b.val() >= 2:
                        sp.wait_ge(res_ready, b.count(-2))
                    sp.dma_start(xr[:, b.par, :, :], tokens(x, b.val())).then_inc(xr_loaded[b.par], DMA)
                b = i.at(2)
                if b.ok(NB):
                    if b.inside or b.val() >= 2:
                        sp.wait_ge(qT_done, b.count(-2))
                    sp.dma_start(qns[:, b.par:b.par + 1, :, :], qn_all[:, bass.ds(b.val(), 1), :, :])\
                      .then_inc(qn_loaded[b.par], DMA)

            for r in range(2):
                sp.wait_ge(q_saved[r], DMA * NB // 2)
            run_steps(sp, step3, -2, LAST3 + 1, LO3, HI3)
            for r in range(2):
                sp.wait_ge(stored[r], DMA * NB // 2)

        @block.gpsimd
        def _(pool):
            def select(out_, compare, base, pattern, channel):
                return pool.affine_select(out=out_, in_=out_, compare_op=compare, fill=0.0, base=base,
                                          pattern=pattern, channel_multiplier=channel)

            pool.memset(ident[:, :], 1.0)
            pool.memset(mask16[:, :], 1.0)
            pool.memset(sel[:, :, :], 1.0)
            pool.memset(bias3[:, :], 0.0)
            pool.memset(neg[:, :], -1.0 / C)
            pool.memset(pos[:, :], 1.0 / C)
            pool.memset(one[:, :], 1.0)
            pool.memset(lnshift[:, :], 0.5 * LN_SHIFT * math.log(2.0)).then_inc(pool_const, 1)
            pool.wait_ge(pool_const, 1)
            select(ident[:, :], ALU.is_equal, 0, [[-1, P]], 1).then_inc(ident_const, 1)
            pool.wait_ge(ident_const, 1)
            for n, lo in enumerate((0, 32, 64)):
                hi = min(lo + 32, K3)
                select(sel[lo:hi, :, :], ALU.is_equal, 0, [[-1, E], [0, NB]], 1).then_inc(sel_const, 1)
                pool.wait_ge(sel_const, n + 1)
            select(mask16[:, :], ALU.is_ge, 0, [[-D, H]], 1).then_inc(pool_const, 1)
            pool.wait_ge(pool_const, 2)
            select(mask16[:, :], ALU.is_ge, D - 1, [[D, H]], -1).then_inc(pool_const, 1)
            pool.wait_ge(ld_bias, BIAS_DMAS * DMA)
            pool.tensor_tensor(bsrc[:, 2 * F + C:], bsrc[:, 2 * F + C:], dbo16, ALU.add).then_inc(split_pool, 1)
            pool.wait_ge(split_act, 1)
            pool.tensor_tensor(bsrc, bsrc, bias3[0:E, :], ALU.subtract).then_inc(split_pool, 1)
            pool.wait_ge(split_act, 3)
            pool.tensor_tensor(bsrc, bsrc, bmid, ALU.subtract).then_inc(split_pool, 1)

            def step(i):
                b = i.at(2)
                if b.ok(NB):
                    p = b.par
                    pool.wait_ge(rinv_ready, b.count())
                    pool.wait_ge(mv_done, b.count())
                    if b.inside or b.val() >= 2:
                        pool.wait_ge(xT_done, b.count(-2))
                    pool.tensor_tensor(xn[:, p, :, :], xin[:, p, :, :], mv[:, p, :, 0:1].to_broadcast([P, T, C]),
                                       ALU.subtract).then_inc(xm_ready, 1)
                    pool.wait_ge(xm_ready, b.count())
                    pool.tensor_tensor(xn[:, p, :, :], xn[:, p, :, :],
                                       rinv[:, 1 - p, NR:NR + T].unsqueeze(2).to_broadcast([P, T, C]), ALU.mult)\
                        .then_inc(xn_ready, 1)
                b = i.at(-1)
                if b.ok(NB):
                    p = b.par
                    pool.wait_ge(rsum_ready, b.count())
                    v = pr[:, p, :].rearrange("p (k n) -> p k n", k=HC)
                    pool.tensor_tensor(v, v, rsum[:, p, :].unsqueeze(2).to_broadcast([P, HC, N]), ALU.mult)\
                        .then_inc(p_ready, 1)

            run_steps(pool, step, FIRST1, LAST1, LO1, HI1)

            heads = mask16[:, :].unsqueeze(2).to_broadcast([P, H, E])

            def step3(i):
                b = i.at(-1)
                if b.ok(NB):
                    p = b.par
                    pool.wait_ge(rden_ready, b.count())
                    v = pr[:, p, :].rearrange("p (h e) -> p h e", e=E)
                    pool.tensor_tensor(v, v, rden[:, p, :].unsqueeze(2).to_broadcast([P, T * H, E]), ALU.mult)\
                        .then_inc(p3_ready, 1)
                b = i.at(1)
                if b.ok(NB):
                    p = b.par
                    if b.inside or b.val() >= 2:
                        pool.wait_ge(s3_done, b.count(-2))
                        pool.wait_ge(vw_done, b.count(-2))
                    for blk, src, ready in ((kblk, kT, kblk_ready), (vblk, vT, vblk_ready)):
                        s = src[:, :, bass.ds(b.val(), 1)].rearrange("p e o -> p o e").to_broadcast([P, H, E])
                        pool.tensor_tensor(blk[:, p, :].rearrange("p (h e) -> p h e", h=H), s, heads, ALU.mult)\
                            .then_inc(ready, 1)

            pool.wait_ge(e_kv_ready, 2)
            run_steps(pool, step3, FIRST3, LAST3, LO3, HI3)

        @block.scalar
        def _(act):
            def rest(dst, name):
                act.dma_start(dst, a[name]).then_inc(ld_rest, DMA)

            rest(pW[:, :], "L0_attn_proj_w")
            rest(gb16[:, 0, :], "L0_ffn_e_ln_g")
            rest(gb16[:, 1, :], "L0_ffn_e_ln_b")
            rest(dWo[:, :], "L0_ffn_d_Wo")
            rest(cWk[:, :], "L0_ffn_c_Wk")
            rest(cWv[:, :], "L0_ffn_c_Wv")
            rest(cWo[:, :], "L0_ffn_c_Wo")

            def bias(dst, src):
                act.dma_start(dst, src).then_inc(ld_bias, DMA)

            bias(bsrc[:, 0:F], a["L0_ffn_e_b1"])
            bias(bsrc[:, F:2 * F], a["L0_ffn_e_bg"])
            bias(bsrc[:, 2 * F:2 * F + C], a["L0_ffn_e_b2"])
            bias(bsrc[:, 2 * F + C:], a["L0_ffn_slot_query"][0])
            bias(dbo16, a["L0_ffn_d_bo"].partition_broadcast(E))
            act.preload_act_table_set("natural_log_exp_and_others")
            act.wait_ge(pool_const, 1)
            act.wait_ge(x_loaded[1], DMA)
            for g in range(RING):
                expert_group(act, g, ld_exp)
            act.wait_ge(pool_const, 3)
            act.wait_ge(split_pool, 1)
            act.activation(bias3[0:E, :], bsrc, ACT.Copy).then_inc(split_act, 1)
            act.wait_ge(split_pool, 2)
            act.activation(bmid, bsrc, ACT.Copy).then_inc(split_act, 1)
            act.activation(bias3[32:32 + E, :], bsrc, ACT.Copy).then_inc(split_act, 1)
            act.wait_ge(split_pool, 3)
            act.activation(bias3[64:64 + E, :], bsrc, ACT.Copy).then_inc(split_act, 1)

            def step(i):
                b = i.at(0)
                if b.ok(NB):
                    p = b.par
                    act.wait_ge(qkv_done, b.count())
                    if b.inside or b.val() >= 1:
                        act.wait_ge(ssum_done, b.count(-1))
                    act.activation(sq[:, :, :], psB[:, p, :, 0:2 * C], ACT.Square).then_inc(sq_ready, 1)
                b = i.at(1)
                if b.ok(NB):
                    p = b.par
                    act.wait_ge(xT_done, b.count())
                    if b.inside or b.val() >= 2:
                        act.wait_ge(scores_done, b.count(-2))
                        act.wait_ge(xT_saved[p], b.dmas(-2))
                    if i.at(-2).ok(NB):
                        act.wait_ge(m_done, i.count(-2))
                    act.activation(xnT[:, p, :], psX[:, 0:N], ACT.Copy, bias=1.0).then_inc(xT_ready, 1)
                b = i.at(-2)
                if b.ok(NB):
                    act.wait_ge(m_done, b.count())
                    act.activation(M_all[:, bass.ds(b.val(), 1), :], psX[:, N:N + C].unsqueeze(1), ACT.Copy)\
                       .then_inc(m_ready, 1)
                b = i.at(0)
                if b.ok(NB):
                    p = b.par
                    if b.inside or b.val() >= 2:
                        act.wait_ge(slot_done, b.count(-2))
                    act.activation(vv[:, p, :, :], psB[:, p, :, 2 * C:4 * C], ACT.Copy).then_inc(v_ready, 1)
                lo = 0 if i.ok(NB) else NR
                hi = NR + T if i.at(3).ok(NB) else NR
                if lo < hi:
                    p = i.par
                    if i.ok(NB):
                        act.wait_ge(ss_ready, i.count())
                    if i.at(3).ok(NB):
                        act.wait_ge(var_ready, i.count(3))
                    act.activation(lnb[:, lo:hi], small[:, p, lo:hi], ACT.Ln,
                                   scale=-2.0 ** (LN_SHIFT + 1))\
                       .then_inc(ln_done, 1)
                    act.wait_ge(ln_done, i.count(3))
                    act.activation(rinv0[:, p, lo:hi], lnb[:, lo:hi], ACT.Exp, scale=-0.5,
                                   bias=lnshift[:, 0:1]).then_inc(rinv0_ready, 1)
                b = i.at(-1)
                if b.ok(NB):
                    p = b.par
                    act.wait_ge(pT_done, b.count())
                    if b.inside or b.val() >= 2:
                        act.wait_ge(slot_done, b.count(-2))
                    act.activation(prT[:, p, :], psT[:, :], ACT.Copy).then_inc(pT_ready, 1)
                b = i.at(0)
                if b.ok(NB):
                    p = b.par
                    act.wait_ge(max_ready, b.count())
                    if b.inside or b.val() >= 2:
                        act.wait_ge(pT_done, b.count(-2))
                    for k in range(HC):
                        last = act.activation(pr[:, p, k * N:(k + 1) * N], psS[:, k * N:(k + 1) * N], ACT.Exp,
                                              bias=nmax[:, p, k:k + 1], accum_out=ssum[:, p, k:k + 1])
                    last.then_inc(exp_ready, 1)

            run_steps(act, step, FIRST1, LAST1, LO1, HI1)

            for g in range(NG):
                act.wait_ge(e_o, g + 1)
                act.activation(o_tm[:, g, :], psE[:, g * C:(g + 1) * C], ACT.Copy).then_inc(e_o_ready, 1)
            act.wait_ge(e_var_ready, 1)
            act.activation(lnb[:, 0:NG], small[:, 0, 0:NG], ACT.Ln, scale=-2.0).then_inc(e_ln_done, 1)
            act.wait_ge(e_ln_done, 1)
            act.activation(rinv0[:, 0, 0:NG], lnb[:, 0:NG], ACT.Exp, scale=-0.5).then_inc(e_rinv0_ready, 1)
            act.preload_act_table(ACT.Silu)
            for r in range(2):
                act.wait_ge(q_saved[r], DMA * NB // 2)

            def silu(g):
                if g:
                    act.wait_ge(e_ug_ready, g)
                act.wait_ge(e_u_done, g + 1)
                act.activation(silu_u, psU[:, g % 2, :], ACT.Silu)
                act.wait_ge(e_g_done, g + 1)
                act.activation(silu_g, psG[:, g % 2, :], ACT.Silu).then_inc(e_silu_ready, 1)

            silu(0)
            for g in range(NG):
                if g + 1 < NG:
                    silu(g + 1)
                act.wait_ge(e_ugT_done, g + 1)
                if g:
                    act.wait_ge(e_y_done, g)
                act.activation(ugT, psT[:, :], ACT.Copy).then_inc(e_ugT_ready, 1)
            act.preload_act_table_set("natural_log_exp_and_others")
            act.wait_ge(e_oT_done, 1)
            act.activation(oT, psX[:, :], ACT.Copy).then_inc(e_oT_ready, 1)

            def step3(i):
                b = i.at(1)
                if b.ok(NB):
                    p = b.par
                    act.wait_ge(cq_done, b.count())
                    if b.inside or b.val() >= 2:
                        act.wait_ge(s3_done, b.count(-2))
                    act.activation(cqT[:, p, :], psX[:, 0:N], ACT.Copy).then_inc(cq_ready, 1)
                b = i.at(-2)
                if b.ok(NB):
                    p = b.par
                    act.wait_ge(p3T_done, b.count())
                    if b.inside or b.val() >= 2:
                        act.wait_ge(out_done, b.count(-2))
                    act.activation(prT[:, p, :], psT[:, :], ACT.Copy).then_inc(p3T_ready, 1)
                b = i.at(0)
                if b.ok(NB):
                    p = b.par
                    act.wait_ge(sub_ready, b.count())
                    act.activation(pr[:, p, :], pr[:, p, :], ACT.Exp, scale=SC).then_inc(exp3_ready, 1)
                    act.wait_ge(qT_done, b.count())
                    if b.inside or b.val() >= 2:
                        act.wait_ge(out_done, b.count(-2))
                    act.activation(qT[:, p, :], psK[:, 0:N], ACT.Copy).then_inc(qT_ready, 1)

            run_steps(act, step3, FIRST3, LAST3, LO3, HI3)

        @block.vector
        def _(dve):
            dve.wait_ge(pool_const, 3)
            dve.tensor_copy(bmask[:, :].rearrange("p (h d) -> p h d", h=H),
                            mask16[:, :].unsqueeze(2).to_broadcast([P, H, D])).then_inc(dve_const, 1)
            dve.tensor_reduce(mask4[:, :], mask16[:, :].rearrange("p (j h) -> p h j", h=G), AX_X, ALU.add)\
               .then_inc(dve_const, 1)
            dve.wait_ge(pe_setup, 1)
            dve.tensor_copy(setup_wkT, psC[:, 0:C])
            dve.tensor_copy(setup_sqT, psC[:, C:C + E])
            dve.tensor_copy(gbT[:, :, :], psC[:, C + E:C + 3 * E].rearrange("p (k e) -> p k e", k=2))
            dve.wait_ge(ld_fold, FOLD_DMAS * DMA)
            dve.memset(setup_bk, 1.0 / C).then_inc(dve_setup, 1)
            dve.wait_ge(dve_setup, 1)
            dve.tensor_scalar(setup_bk, setup_bk, cols[:, 1:2], None, ALU.mult).then_inc(dve_setup, 1)
            dve.wait_ge(pe_setup, 2)
            dve.tensor_scalar(setup_q, psX[:, 0:E], cols[:, 0:1], SC, ALU.add, ALU.mult).then_inc(dve_setup, 1)
            dve.wait_ge(dve_setup, 3)
            dve.tensor_tensor(setup_qblk.rearrange("p (h e) -> p h e", h=H),
                              setup_q.unsqueeze(1).to_broadcast([P, H, E]),
                              mask16[:, :].unsqueeze(2).to_broadcast([P, H, E]), ALU.mult).then_inc(dve_setup, 1)
            dve.wait_ge(pe_setup, 3)
            dve.tensor_tensor(WB[:, 0:4 * C], WB[:, 0:4 * C], psU[:, 0, :], ALU.add)
            dve.tensor_tensor(WB[:, 4 * C:5 * C], WB[:, 4 * C:5 * C], psG[:, 0, 0:C], ALU.add).then_inc(dve_setup, 1)
            dve.tensor_scalar(outb[:, :], psU[:, 1, 0:C], 1.0 / H, None, ALU.mult).then_inc(dve_setup, 1)
            dve.wait_ge(pe_setup, 4)
            dve.tensor_copy(Wslot[:, :], psS[:, 0:HS]).then_inc(dve_setup, 1)
            dve.wait_ge(pe_setup, 5)
            dve.tensor_tensor(Wslot[:, :], Wslot[:, :], psT[:, 0:HS], ALU.add).then_inc(dve_setup, 1)

            def step(i):
                b = i.at(3)
                if b.ok(NB):
                    p = b.par
                    dve.wait_ge(x_loaded[p], b.dmas())
                    for t in range(T):
                        last = dve.bn_stats(bnst[:, p, t, :], xin[:, p, t, :])
                    last.then_inc(bn_done, 1)
                    dve.wait_ge(bn_done, b.count())
                b = i.at(-1)
                if b.ok(NB):
                    p = b.par
                    dve.wait_ge(rinv_ready, b.count(3))
                    dve.wait_ge(v_ready, b.count())
                    if b.inside or b.val() >= 2:
                        dve.wait_ge(kv_done, b.count(-2))
                        dve.wait_ge(q_saved[p], b.dmas(-2))
                    for t in range(T):
                        last = dve.tensor_tensor(
                            qk[:, p, t, :].rearrange("p (h d) -> p h d", d=D),
                            psB[:, p, t, 0:2 * C].rearrange("p (h d) -> p h d", d=D),
                            rinv[:, p, t * 2 * H:(t + 1) * 2 * H].unsqueeze(2).to_broadcast([P, 2 * H, D]), ALU.mult)
                    last.then_inc(qk_ready, 1)
                b = i.at(-1)
                if b.ok(NB):
                    dve.wait_ge(exp_ready, b.count())
                    dve.reciprocal(rsum[:, b.par, :], ssum[:, b.par, :]).then_inc(rsum_ready, 1)
                b = i.at(3)
                if b.ok(NB):
                    p = b.par
                    for t in range(T):
                        last = dve.bn_aggr(mv[:, p, t, :], bnst[:, p, t, :])
                    last.then_inc(mv_done, 1)
                b = i.at(0)
                if b.ok(NB):
                    dve.wait_ge(sq_ready, b.count())
                    if b.inside or b.val() >= 1:
                        dve.wait_ge(ss_ready, b.count(-1))
                    dve.tensor_reduce(ssq[:, :], sq[:, :, :].rearrange("p t (h d) -> p (t h) d", d=D), AX_X,
                                      ALU.add).then_inc(ssum_done, 1)
                b = i.at(3)
                if b.ok(NB):
                    dve.wait_ge(mv_done, b.count())
                    dve.tensor_scalar(small[:, i.par, NR:NR + T], mv[:, b.par, :, 1], LN_EPS, -0.5,
                                      ALU.add, ALU.mult)\
                       .then_inc(var_ready, 1)
                b = i.at(0)
                if b.ok(NB):
                    dve.wait_ge(ssum_done, b.count())
                    dve.tensor_scalar(small[:, b.par, 0:NR], ssq[:, :], L2_GUARD, -0.5, ALU.max, ALU.mult)\
                       .then_inc(ss_ready, 1)
                b = i.at(-2)
                if b.ok(NB):
                    dve.wait_ge(slot_done, b.count())
                    if b.inside or b.val() >= 1:
                        dve.wait_ge(slot_ready, b.count(-1))
                    dve.tensor_tensor(rm[:, :, :], psC[:, C:C + G * E].rearrange("p (h e) -> p h e", h=G),
                                      mask4[:, :].unsqueeze(2).to_broadcast([P, G, E]), ALU.mult)\
                       .then_inc(slot_masked, 1)
                b = i.at(0)
                if b.ok(NB):
                    dve.wait_ge(scores_done, b.count())
                    dve.tensor_reduce(nmax[:, b.par, :], psS[:, :].rearrange("p (k n) -> p k n", k=HC), AX_X,
                                      ALU.max, negate=True).then_inc(max_ready, 1)
                lo = 0 if i.ok(NB) else NR
                hi = NR + T if i.at(3).ok(NB) else NR
                y = rinv0[:, i.par, lo:hi]
                if lo < hi:
                    dve.wait_ge(rinv0_ready, i.count(3))
                    dve.tensor_tensor(nwt[:, 0, lo:hi], y, y, ALU.mult).then_inc(newton1, 1)
                b = i.at(-2)
                if b.ok(NB):
                    dve.wait_ge(slot_masked, b.count())
                    dve.tensor_reduce(slots[:, :, bass.ds(b.val(), 1)],
                                      rm[:, :, :].rearrange("p h e -> p e h"), AX_X, ALU.add).then_inc(slot_ready, 1)
                if lo < hi:
                    dve.wait_ge(newton1, i.count(3))
                    dve.tensor_tensor(nwt[:, 1, lo:hi], nwt[:, 0, lo:hi], small[:, i.par, lo:hi], ALU.mult)\
                       .then_inc(newton2, 1)
                b = i.at(-1)
                if b.ok(NB):
                    dve.wait_ge(kv_done, b.count())
                    dve.tensor_tensor(kvm[:, b.par, :], psC[:, 0:C], bmask[:, :], ALU.mult).then_inc(kvm_ready, 1)
                if lo < hi:
                    dve.wait_ge(newton2, i.count(3))
                    dve.scalar_tensor_tensor(rinv[:, i.par, lo:hi], nwt[:, 1, lo:hi], 1.5, y, ALU.add, ALU.mult)\
                       .then_inc(rinv_ready, 1)

            run_steps(dve, step, FIRST1, LAST1, LO1, HI1)

            for g in range(NG):
                dve.wait_ge(e_o_ready, g + 1)
                last = dve.bn_stats(bnst[:, g // 2, g % 2, :], o_tm[:, g, :])
            last.then_inc(bn_done, 1)
            dve.wait_ge(bn_done, NB + 1)
            for g in range(NG):
                last = dve.bn_aggr(mv[:, g // 2, g % 2, :], bnst[:, g // 2, g % 2, :])
            last.then_inc(mv_done, 1)
            dve.wait_ge(mv_done, NB + 1)
            half_v, y0 = small[:, 0, 0:NG], rinv0[:, 0, 0:NG]
            dve.tensor_scalar(half_v, mv[:, :, :, 1].rearrange("p a t -> p (a t)"), LN_EPS, -0.5, ALU.add, ALU.mult)\
               .then_inc(e_var_ready, 1)
            dve.wait_ge(e_rinv0_ready, 1)
            dve.tensor_tensor(nwt[:, 0, 0:NG], y0, half_v, ALU.mult).then_inc(e_newton, 1)
            dve.wait_ge(e_newton, 1)
            dve.tensor_tensor(nwt[:, 1, 0:NG], nwt[:, 0, 0:NG], y0, ALU.mult).then_inc(e_newton, 1)
            dve.wait_ge(e_newton, 2)
            dve.scalar_tensor_tensor(rinv[:, 0, 0:NG], nwt[:, 1, 0:NG], 1.5, y0, ALU.add, ALU.mult)\
               .then_inc(e_newton, 1)
            dve.wait_ge(e_newton, 3)
            for g in range(NG):
                dve.tensor_scalar(hn[:, g, :], o_tm[:, g, :], mv[:, g // 2, g % 2, 0:1], rinv[:, 0, g:g + 1],
                                  ALU.subtract, ALU.mult).then_inc(e_hn_ready, 1)
            h3 = hT.rearrange("p (e b) -> p e b", e=E)
            hx = psX[:, :].rearrange("p (e b) -> p e b", e=E)
            for g in range(NG):
                eg = slice(g * G, (g + 1) * G)
                dve.wait_ge(e_hnT_done, NG)
                dve.tensor_tensor(h3[:, eg, :], hx[:, eg, :], gbT[:, 0, eg].unsqueeze(2).to_broadcast([P, G, NB]),
                                  ALU.mult).then_inc(e_hg_done, 1)
                dve.wait_ge(e_hg_done, g + 1)
                dve.tensor_tensor(h3[:, eg, :], h3[:, eg, :], gbT[:, 1, eg].unsqueeze(2).to_broadcast([P, G, NB]),
                                  ALU.add).then_inc(e_h_ready, 1)
            for g in range(NG):
                dve.wait_ge(e_silu_ready, g + 1)
                if g:
                    dve.wait_ge(e_ugT_done, g)
                dve.tensor_tensor(ug, silu_u, silu_g, ALU.mult).then_inc(e_ug_ready, 1)
                if g:
                    dve.wait_ge(e_y_done, g)
                    dve.tensor_tensor(o2_tm[:, g - 1, :], psY[:, 0:C], o_tm[:, g - 1, :], ALU.add)\
                       .then_inc(e_o2_ready, 1)
            dve.wait_ge(e_y_done, NG)
            dve.tensor_tensor(o2_tm[:, NG - 1, :], psY[:, 0:C], o_tm[:, NG - 1, :], ALU.add).then_inc(e_o2_ready, 1)
            dve.wait_ge(e_kv_done, 1)
            dve.tensor_scalar(kT[:, :, :].rearrange("p e b -> p (e b)"), psU[:, 0, :], cols[:, 2:3], None, ALU.add)\
               .then_inc(e_kv_ready, 1)
            dve.wait_ge(e_kv_done, 2)
            dve.tensor_scalar(vT[:, :, :].rearrange("p e b -> p (e b)"), psG[:, 0, :], cols[:, 3:4], None, ALU.add)\
               .then_inc(e_kv_ready, 1)

            def step3(i):
                b = i.at(0)
                if b.ok(NB):
                    p = b.par
                    s3 = psS[:, :].rearrange("p (h e) -> p h e", e=E)
                    dve.wait_ge(s3_done, b.count())
                    dve.tensor_reduce(top, s3, AX_X, ALU.max).then_inc(top_ready, 1)
                    dve.wait_ge(top_ready, b.count())
                    if b.inside or b.val() >= 2:
                        dve.wait_ge(p3T_done, b.count(-2))
                    dve.tensor_tensor(pr[:, p, :].rearrange("p (h e) -> p h e", e=E), s3,
                                      top.unsqueeze(2).to_broadcast([P, T * H, E]), ALU.subtract)\
                       .then_inc(sub_ready, 1)
                b = i.at(-1)
                if b.ok(NB):
                    p = b.par
                    dve.wait_ge(exp3_ready, b.count())
                    if b.inside or b.val() >= 1:
                        dve.wait_ge(rden_ready, b.count(-1))
                    dve.tensor_reduce(den, pr[:, p, :].rearrange("p (h e) -> p h e", e=E), AX_X, ALU.add)\
                       .then_inc(den_ready, 1)
                    dve.wait_ge(den_ready, b.count())
                    dve.reciprocal(rden[:, p, :], den).then_inc(rden_ready, 1)
                b = i.at(-3)
                if b.ok(NB):
                    p = b.par
                    dve.wait_ge(out_done, b.count())
                    dve.wait_ge(xr_loaded[p], b.dmas())
                    if b.inside or b.val() >= 2:
                        dve.wait_ge(stored[p], b.dmas(-2))
                    dve.tensor_tensor(res[:, p, :, :], psO[:, p, 0:N].rearrange("p (t c) -> p t c", t=T),
                                      xr[:, p, :, :], ALU.add).then_inc(res_ready, 1)
                b = i.at(0)
                if b.ok(NB):
                    p = b.par
                    dve.wait_ge(vw_done, b.count())
                    if b.inside or b.val() >= 2:
                        dve.wait_ge(out_done, b.count(-2))
                    dve.tensor_tensor(vw[:, p, :, :], psV[:, 0:N].rearrange("p (k c) -> p k c", k=HC),
                                      outb[:, :].unsqueeze(1).to_broadcast([P, HC, C]), ALU.add).then_inc(vw_ready, 1)
            run_steps(dve, step3, 0, LAST3 + 1, LO3, HI3)

        @block.tensor
        def _(pe):
            pe.wait_ge(ld_fold, FOLD_DMAS * DMA)
            pe.wait_ge(ld_rest, REST_DMAS * DMA)
            pe.wait_ge(pool_const, 3)
            pe.transpose(psC[:, 0:C], setup_wk, ident[:, :])
            pe.transpose(psC[:, C:C + E], sq16[:, :], ident[0:E, 0:E])
            for k in range(2):
                last = pe.transpose(psC[:, C + (k + 1) * E:C + (k + 2) * E], gb16[:, k, :], ident[0:E, 0:E])
            last.then_inc(pe_setup, 1)
            for dst, lo, hi in ((psU[:, 0, :], 0, 4 * C), (psG[:, 0, 0:C], 4 * C, 5 * C)):
                pe.matmul(dst, neg[:, :], WB[:, lo:hi], start=True, stop=False)
                pe.matmul(dst, pos[:, :], rows[:, lo:hi], start=False, stop=True)
            pe.wait_ge(dve_setup, 1)
            pe.matmul(psX[:, 0:E], setup_wq, setup_sqT, start=True, stop=True).then_inc(pe_setup, 1)
            for k in range(2):
                last = pe.matmul(psU[:, 1, 0:C], one[:, :], rows[:, (6 + k) * C:(7 + k) * C], start=(k == 0), stop=(k == 1))
            last.then_inc(pe_setup, 1)
            pe.wait_ge(dve_setup, 4)
            pe.matmul(psS[:, 0:HS], setup_wkT, setup_qblk, start=True, stop=True).then_inc(pe_setup, 1)
            pe.wait_ge(dve_setup, 7)
            pe.matmul(psT[:, 0:HS], neg[:, :], Wslot[:, :], start=True, stop=False)
            pe.matmul(psT[:, 0:HS], setup_bk, setup_qblk, start=False, stop=True).then_inc(pe_setup, 1)
            pe.wait_ge(dve_setup, 8)

            def step(i):
                def project(t):
                    b = i.at(0)
                    p = b.par
                    if t == 0:
                        pe.wait_ge(xT_ready, b.count())
                        if b.inside or b.val() >= 2:
                            pe.wait_ge(qk_ready, b.count(-2))
                    return pe.matmul(psB[:, p, t, :], xnT[:, p, t * P:(t + 1) * P], WB[:, 0:4 * C],
                                     start=True, stop=True)

                if i.ok(NB):
                    project(0)
                    project(1).then_inc(qkv_done, 1)
                b = i.at(1)
                if b.ok(NB):
                    p = b.par
                    pe.wait_ge(xn_ready, b.count())
                    if b.inside or b.val() >= 1:
                        pe.wait_ge(xT_ready, b.count(-1))
                    if i.at(-3).ok(NB):
                        pe.wait_ge(m_ready, i.count(-3))
                    for t in range(T):
                        last = pe.transpose(psX[:, t * P:(t + 1) * P], xn[:, p, t, :], ident[:, :])
                    last.then_inc(xT_done, 1)
                b = i.at(-2)
                if b.ok(NB):
                    p = b.par
                    pe.wait_ge(kvm_ready, b.count())
                    if b.inside or b.val() >= 1:
                        pe.wait_ge(m_ready, b.count(-1))
                    pe.matmul(psX[:, N:N + C], kvm[:, p, :], pW[:, :], start=True, stop=True).then_inc(m_done, 1)
                    pe.wait_ge(pT_ready, b.count())
                    for j in range(4):
                        for t in range(T):
                            last = pe.matmul(psC[32 * j:32 * j + 32, C:C + G * E],
                                             vv[:, p, t, C + 32 * j:C + 32 * j + 32],
                                             prT[:, p, t * HS + j * G * E:t * HS + (j + 1) * G * E],
                                             start=(t == 0), stop=(t == T - 1))
                    last.then_inc(slot_done, 1)
                b = i.at(0)
                if b.ok(NB):
                    if b.inside or b.val() >= 1:
                        pe.wait_ge(exp_ready, b.count(-1))
                    for k in range(HC):
                        last = pe.matmul(psS[:, k * N:(k + 1) * N], Wslot[:, k * P:(k + 1) * P], xnT[:, b.par, :],
                                         start=True, stop=True)
                    last.then_inc(scores_done, 1)
                b = i.at(-1)
                if b.ok(NB):
                    p = b.par
                    pe.wait_ge(p_ready, b.count())
                    if b.inside or b.val() >= 1:
                        pe.wait_ge(pT_ready, b.count(-1))
                    for t in range(T):
                        for k in range(HC):
                            last = pe.transpose(psT[:, t * HS + k * P:t * HS + (k + 1) * P],
                                                pr[:, p, k * N + t * P:k * N + (t + 1) * P], ident[:, :])
                    last.then_inc(pT_done, 1)
                    pe.wait_ge(qk_ready, b.count())
                    if b.inside or b.val() >= 1:
                        pe.wait_ge(slot_masked, b.count(-1))
                    for t in range(T):
                        last = pe.matmul(psC[:, 0:C], vv[:, p, t, 0:C], qk[:, p, t, C:2 * C],
                                         start=(t == 0), stop=(t == T - 1))
                    last.then_inc(kv_done, 1)

            run_steps(pe, step, -1, LAST1, LO1, HI1)

            def bias(dst, g, lo, n):
                pe.matmul(dst, sel[:, g * G:(g + 1) * G, :].rearrange("p e b -> p (e b)"), bias3[:, lo:lo + n],
                          start=True, stop=False, skip_group_check=True)

            pe.wait_ge(slot_ready, NB)
            pe.wait_ge(split_act, 4)
            for g in range(NG):
                if g:
                    pe.wait_ge(e_o_ready, g)
                bias(psE[:, g * C:(g + 1) * C], g, 2 * F + C, C)
                pe.matmul(psE[:, g * C:(g + 1) * C], slots[:, g * G:(g + 1) * G, :].rearrange("p e b -> p (e b)"),
                          dWo[:, :], start=False, stop=True, skip_group_check=True).then_inc(e_o, 1)
            for g in range(NG):
                pe.wait_ge(e_hn_ready, g + 1)
                pe.transpose(psX[:, g * C:(g + 1) * C], hn[:, g, :], ident[:, :]).then_inc(e_hnT_done, 1)
            pe.wait_ge(ld_exp, RING * PER_GROUP)

            def up(g, ps_, w, lo, done):
                pe.wait_ge(e_h_ready, g + 1)
                if g >= RING:
                    pe.wait_ge(ld_exp2, (g - RING + 1) * PER_GROUP)
                if g >= 2:
                    pe.wait_ge(e_silu_ready, g - 1)
                dst = ps_[:, g % 2, :]
                bias(dst, g, lo, F)
                for j in range(G):
                    e = g * G + j
                    last = pe.matmul(dst[NB * j:NB * (j + 1), :], hT[:, e * NB:(e + 1) * NB], w[:, g % RING, j, :],
                                     start=False, stop=True, skip_group_check=True)
                last.then_inc(done, 1)

            def turn(g):
                pe.wait_ge(e_ug_ready, g + 1)
                if g:
                    pe.wait_ge(e_ugT_ready, g)
                for k in range(FK):
                    last = pe.transpose(psT[:, k * P:(k + 1) * P], ug[:, k * P:(k + 1) * P], ident[:, :])
                last.then_inc(e_ugT_done, 1)

            def down(g):
                pe.wait_ge(e_ugT_ready, g + 1)
                if g:
                    pe.wait_ge(e_o2_ready, g)
                bias(psY[:, 0:C], g, 2 * F, C)
                for k in range(FK):
                    for j in range(G):
                        last = pe.matmul(psY[NB * j:NB * (j + 1), 0:C], ugT[:, k * P + NB * j:k * P + NB * (j + 1)],
                                         W2[:, g % RING, j, k, :], start=False, stop=(k == FK - 1),
                                         skip_group_check=True)
                last.then_inc(e_y_done, 1)

            for g in range(2):
                up(g, psU, W1, 0, e_u_done)
                up(g, psG, Wg, F, e_g_done)
            for g in range(NG):
                turn(g)
                if g + 2 < NG:
                    up(g + 2, psU, W1, 0, e_u_done)
                down(g)
                if g + 2 < NG:
                    up(g + 2, psG, Wg, F, e_g_done)
            for g in range(NG):
                pe.wait_ge(e_o2_ready, g + 1)
                last = pe.transpose(psX[:, g * C:(g + 1) * C], o2_tm[:, g, :], ident[:, :])
            last.then_inc(e_oT_done, 1)
            pe.wait_ge(e_oT_ready, 1)
            pe.matmul(psU[:, 0, :], cWk[:, :], oT, start=True, stop=True).then_inc(e_kv_done, 1)
            pe.matmul(psG[:, 0, :], cWv[:, :], oT, start=True, stop=True).then_inc(e_kv_done, 1)

            pe.wait_ge(m_ready, NB)
            for r in range(2):
                pe.wait_ge(xT_saved[r], DMA * NB // 2)
            pe.wait_ge(e_kv_ready, 2)

            def step3(i):
                b = i.at(0)
                if b.ok(NB):
                    p = b.par
                    pe.wait_ge(cq_ready, b.count())
                    pe.wait_ge(kblk_ready, b.count())
                    if b.inside or b.val() >= 1:
                        pe.wait_ge(sub_ready, b.count(-1))
                    for t in range(T):
                        last = pe.matmul(psS[:, t * HS:(t + 1) * HS], cqT[:, p, t * P:(t + 1) * P], kblk[:, p, :],
                                         start=True, stop=True)
                    last.then_inc(s3_done, 1)
                b = i.at(-2)
                if b.ok(NB):
                    p = b.par
                    pe.wait_ge(p3_ready, b.count())
                    if b.inside or b.val() >= 1:
                        pe.wait_ge(p3T_ready, b.count(-1))
                    for k in range(HC):
                        for t in range(T):
                            last = pe.transpose(psT[:, k * N + t * P:k * N + (t + 1) * P],
                                                pr[:, p, t * HS + k * P:t * HS + (k + 1) * P], ident[:, :])
                    last.then_inc(p3T_done, 1)
                b = i.at(1)
                if b.ok(NB):
                    if b.inside or b.val() >= 1:
                        pe.wait_ge(cq_ready, b.count(-1))
                    pe.matmul(psX[:, 0:N], WB[:, 4 * C:5 * C],
                              xnT_all[:, bass.ds(b.val(), 1), :].rearrange("p o n -> p (o n)"),
                              start=True, stop=True).then_inc(cq_done, 1)
                b = i.at(0)
                if b.ok(NB):
                    p = b.par
                    pe.wait_ge(vblk_ready, b.count())
                    if b.inside or b.val() >= 1:
                        pe.wait_ge(vw_ready, b.count(-1))
                    for k in range(HC):
                        last = pe.matmul(psV[:, k * C:(k + 1) * C], vblk[:, p, k * P:(k + 1) * P], cWo[:, :],
                                         start=True, stop=True)
                    last.then_inc(vw_done, 1)
                b = i.at(0)
                if b.ok(NB):
                    p = b.par
                    pe.wait_ge(qn_loaded[p], b.dmas())
                    if b.inside or b.val() >= 1:
                        pe.wait_ge(qT_ready, b.count(-1))
                    for t in range(T):
                        last = pe.transpose(psK[:, t * P:(t + 1) * P], qns[:, p, t, :], ident[:, :])
                    last.then_inc(qT_done, 1)
                b = i.at(-2)
                if b.ok(NB):
                    p = b.par
                    pe.wait_ge(p3T_ready, b.count())
                    pe.wait_ge(vw_ready, b.count())
                    pe.wait_ge(qT_ready, b.count())
                    if b.inside or b.val() >= 2:
                        pe.wait_ge(res_ready, b.count(-2))
                    for t in range(T):
                        dst = psO[:, p, t * C:(t + 1) * C]
                        pe.matmul(dst, qT[:, p, t * P:(t + 1) * P],
                                  M_all[:, bass.ds(b.val(), 1), :].rearrange("p o c -> p (o c)"),
                                  start=True, stop=False)
                        for k in range(HC):
                            last = pe.matmul(dst, prT[:, p, k * N + t * P:k * N + (t + 1) * P], vw[:, p, k, :],
                                             start=False, stop=(k == HC - 1))
                    last.then_inc(out_done, 1)

            run_steps(pe, step3, FIRST3, LAST3, LO3, HI3)


def kernel(**inputs):
    import numpy as _np
    import concourse.bacc as _bacc
    from concourse import mybir as _mybir
    from concourse.bass_utils import run_bass_kernel_spmd as _run

    nc = _bacc.Bacc("TRN2", target_bir_lowering=False, num_devices=1)
    arrays, aps = {}, {}
    for name, value in inputs.items():
        v = _np.ascontiguousarray(value)
        arrays[f"in_{name}"] = v
        aps[name] = nc.dram_tensor(f"in_{name}", v.shape, _mybir.dt.from_np(v.dtype), kind="ExternalInput").ap()
    shape = inputs["L0_attn_x"].shape
    out = nc.dram_tensor("out", shape, _mybir.dt.float32, kind="ExternalOutput").ap()
    linear_attention_slot_experts_kernel(nc, aps, out)
    r = _run(nc, [arrays], core_ids=[0])
    return r.results[0]["out"]
```

```python
import math
from contextlib import ExitStack

import concourse.bass as bass
from concourse import mybir

P = 128
F32 = mybir.dt.float32
BF16 = mybir.dt.bfloat16
ALU = mybir.AluOpType
ACT = mybir.ActivationFunctionType
AX_X = mybir.AxisListType.X

LN_EPS = 1e-5
L2_GUARD = 1e-24
LN_SHIFT = 30
DMA = 16


class Step:

    def __init__(self, base, off, inside):
        self.base, self.off, self.inside = base, off, inside

    def at(self, d):
        return Step(self.base, self.off + d, self.inside)

    @property
    def par(self):
        return self.off % 2

    def ok(self, n):
        return self.inside or 0 <= self.base + self.off < n

    def now(self, k):
        return not self.inside and self.base + self.off == k

    def val(self, c=0):
        return self.base + (self.off + c)

    def count(self, c=0):
        return self.base + (self.off + c + 1)

    def dmas(self, c=0):
        return self.base * (DMA // 2) + ((self.off + c - self.par) // 2 + 1) * DMA


def single(i):
    return Step(i - i % 2, i % 2, False)


def run_steps(eng, body, first, last, lo, hi):
    for i in range(first, lo):
        body(single(i))
    with eng.Fori(lo, hi - 1, 2) as i:
        for r in range(2):
            body(Step(i, r, True))
    for i in range(hi, last + 1):
        body(single(i))


def linear_attention_slot_experts_kernel(nc, a, out):
    x = a["L0_attn_x"]
    NB, N, C = x.shape
    H, D = 16, 8
    E, F = a["L0_ffn_e_W1"].shape[0], a["L0_ffn_e_W1"].shape[2]
    T = N // P
    HS = H * E
    HC = HS // P
    G = 4
    NG = E // G
    FK = F // P
    SC = 1.0 / math.sqrt(D)
    K3 = 3 * E
    BJ = P // E
    BW = (2 * F + 2 * C) // BJ
    RING = 3
    NR = 2 * T * H
    FOLD_DMAS, SLOT_DMAS, REST_DMAS, BIAS_DMAS = 4, 5, 12, 5
    assert C == P and T == 2 and HC == 2 and G * NB == P and H * D == C

    ctx = ExitStack()
    with ctx:
        def sb(name, shape, dtype=F32):
            return ctx.enter_context(nc.sbuf_tensor(name, shape, dtype))

        def sem(name):
            return ctx.enter_context(nc.semaphore(name))

        xnT_all = sb("xnT_all", [P, NB, N])
        qn_all = sb("qn_all", [P, NB, T, C])
        M_all = sb("M_all", [P, NB, C])
        W1 = sb("W1", [P, RING, G, F])
        Wg = sb("Wg", [P, RING, G, F])
        W2 = sb("W2", [P, RING, G, FK, C])
        slots = sb("slots", [P, E, NB])
        WB = sb("WB", [P, 5 * C])
        Wslot = sb("Wslot", [P, HS])
        dWo = sb("dWo", [P, C])
        pW = sb("pW", [P, C])
        cWk = sb("cWk", [P, C])
        cWv = sb("cWv", [P, C])
        cWo = sb("cWo", [P, C])
        outb = sb("outb", [P, C])
        cols = sb("cols", [P, 4])
        rows = sb("rows", [1, 3 * C])
        sq16 = sb("sq16", [E, C])
        bias3 = sb("bias3", [K3, BJ * BW], BF16)
        bias_left = sb("bias_left", [P, BW])
        bias_dbo = sb("bias_dbo", [P, C // BJ])
        bias_part = sb("bias_part", [P, 3, BW], BF16)
        gb16 = sb("gb16", [E, 2, C])
        gbT = sb("gbT", [P, 2, E])
        ident = sb("ident", [P, P])
        bmask = sb("bmask", [P, P])
        mask16 = sb("mask16", [P, H])
        mask4 = sb("mask4", [P, G])
        sel = sb("sel", [K3, E, NB], BF16)
        neg = sb("neg", [P, P])
        pos = sb("pos", [1, P])
        one = sb("one", [1, P])
        lnshift = sb("lnshift", [P, 1])
        xin = sb("xin", [P, 2, T, C])
        xn = sb("xn", [P, 2, T, C])
        xnT = sb("xnT", [P, 2, N])
        sq = sb("sq", [P, T, 2 * C])
        vv = sb("vv", [P, 2, T, 2 * C])
        qk = sb("qk", [P, 2, T, 2 * C])
        kvm = sb("kvm", [P, 2, C])
        pr = sb("pr", [P, 2, 2 * N])
        prT = sb("prT", [P, 2, 2 * N])
        rm = sb("rm", [P, G, E])
        bnst = sb("bnst", [P, 2, T, 6])
        mv = sb("mv", [P, 2, T, 2])
        small = sb("small", [P, 2, NR + T])
        ssq = sb("ssq", [P, NR])
        lnb = sb("lnb", [P, NR + T])
        rinv0 = sb("rinv0", [P, 2, NR + T])
        nwt = sb("nwt", [P, 2, NR + T])
        rinv = sb("rinv", [P, 2, NR + T])
        nmax = sb("nmax", [P, 2, HC])
        ssum = sb("ssum", [P, 2, HC])
        rsum = sb("rsum", [P, 2, HC])
        setup_wk, setup_wkT, setup_wq, setup_bk = (pr[:, 0, k * C:(k + 1) * C] for k in range(4))
        setup_sqT, setup_q = rm[:, 0, :], rm[:, 1, :]
        setup_qblk = sq[:, 0, :]
        setup_bb = qk[:, 0, :, :].rearrange("p t c -> p (t c)")
        hT = sq[:, :, :].rearrange("p a c -> p (a c)")
        o_tm = prT[:, 0, :].rearrange("p (g c) -> p g c", g=NG)
        o2_tm = prT[:, 1, :].rearrange("p (g c) -> p g c", g=NG)
        hn = pr[:, 0, :].rearrange("p (g c) -> p g c", g=NG)
        oT = pr[:, 1, :]
        silu_u = qk[:, 0, :, :].rearrange("p t c -> p (t c)")
        silu_g = qk[:, 1, :, :].rearrange("p t c -> p (t c)")
        ug = vv[:, 0, :, :].rearrange("p t c -> p (t c)")
        ugT = vv[:, 1, :, :].rearrange("p t c -> p (t c)")
        kT = sb("kT", [P, E, NB])
        vT = sb("vT", [P, E, NB])
        xr, qns, qT = xin, xn, xnT
        cqT = sq
        kblk, vblk = qk[:, :, 0, :], qk[:, :, 1, :]
        vw = vv[:, :, 0, :].rearrange("p a (k c) -> p a k c", k=HC)
        res = vv[:, :, 1, :].rearrange("p a (t c) -> p a t c", t=T)
        top, den = ssq[:, 0:T * H], lnb[:, 0:T * H]
        rden = rinv[:, :, 0:T * H]

        def ps(name, shape):
            return ctx.enter_context(nc.psum_tensor(name, shape, F32))

        psX = ps("psX", [P, 512])
        psB = ps("psB", [P, 2, T, 512])
        psS = ps("psS", [P, 512])
        psT = ps("psT", [P, 512])
        psC = ps("psC", [P, 512])
        psU, psG = psB[:, :, 0, :], psB[:, :, 1, :]
        psY = psC
        slot_banks = [psS[:, 0:C], psT[:, 0:C], psC[:, 0:C], psX[:, 0:C]]
        kv_parts = ((0, psU[:, 0, :], psG[:, 0, :]), (NG - 1, psS, psT))
        psV, psK = psB[:, 0, 0, :], psB[:, 0, 1, :]
        psO = psB[:, 1, :, :]

        ld_fold = sem("ld_fold")
        ld_slot = sem("ld_slot")
        ld_pW = sem("ld_pW")
        ld_rest = sem("ld_rest")
        ld_exp = sem("ld_exp")
        ld_W1, ld_Wg, ld_W2 = sem("ld_W1"), sem("ld_Wg"), sem("ld_W2")
        ld_bias = sem("ld_bias")
        split_pool = sem("split_pool")
        split_act = sem("split_act")
        pool_const = sem("pool_const")
        ident_const = sem("ident_const")
        sel_const = sem("sel_const")
        bias_moved = sem("bias_moved")
        late_done = sem("late_done")
        late_ready = sem("late_ready")
        dve_const = sem("dve_const")
        pe_setup = sem("pe_setup")
        dve_setup = sem("dve_setup")
        x_loaded = [sem("x_loaded0"), sem("x_loaded1")]
        bn_done = sem("bn_done")
        mv_done = sem("mv_done")
        var_ready = sem("var_ready")
        xm_ready = sem("xm_ready")
        xn_ready = sem("xn_ready")
        m_done = sem("m_done")
        m_ready = sem("m_ready")
        xT_done = sem("xT_done")
        xT_ready = sem("xT_ready")
        xT_saved = [sem("xT_saved0"), sem("xT_saved1")]
        qkv_done = sem("qkv_done")
        v_ready = sem("v_ready")
        sq_ready = sem("sq_ready")
        ssum_done = sem("ssum_done")
        ss_ready = sem("ss_ready")
        ln_done = sem("ln_done")
        rinv0_ready = sem("rinv0_ready")
        newton1 = sem("newton1")
        newton2 = sem("newton2")
        rinv_ready = sem("rinv_ready")
        qk_ready = sem("qk_ready")
        q_saved = [sem("q_saved0"), sem("q_saved1")]
        kv_done = sem("kv_done")
        kvm_ready = sem("kvm_ready")
        slot_done = sem("slot_done")
        slot_masked = sem("slot_masked")
        slot_ready = sem("slot_ready")
        scores_done = sem("scores_done")
        max_ready = sem("max_ready")
        exp_ready = sem("exp_ready")
        rsum_ready = sem("rsum_ready")
        p_ready = sem("p_ready")
        pT_done = sem("pT_done")
        pT_ready = sem("pT_ready")
        e_o = sem("e_o")
        e_o_ready = sem("e_o_ready")
        e_var_ready = sem("e_var_ready")
        e_ln_done = sem("e_ln_done")
        e_rinv0_ready = sem("e_rinv0_ready")
        e_newton = sem("e_newton")
        e_hn_ready = sem("e_hn_ready")
        e_hnT_done = sem("e_hnT_done")
        e_hg_done = sem("e_hg_done")
        e_h_ready = sem("e_h_ready")
        e_u_done = sem("e_u_done")
        e_g_done = sem("e_g_done")
        e_silu_ready = sem("e_silu_ready")
        e_ug_ready = sem("e_ug_ready")
        e_ugT_done = sem("e_ugT_done")
        e_ugT_ready = sem("e_ugT_ready")
        e_y_done = sem("e_y_done")
        e_o2_ready = sem("e_o2_ready")
        e_oT_done = sem("e_oT_done")
        e_oT_ready = sem("e_oT_ready")
        e_kv_done = sem("e_kv_done")
        e_kv_ready = sem("e_kv_ready")
        cq_done = sem("cq_done")
        cq_ready = sem("cq_ready")
        kblk_ready = sem("kblk_ready")
        vblk_ready = sem("vblk_ready")
        s3_done = sem("s3_done")
        top_ready = sem("top_ready")
        sub_ready = sem("sub_ready")
        exp3_ready = sem("exp3_ready")
        den_ready = sem("den_ready")
        rden_ready = sem("rden_ready")
        p3_ready = sem("p3_ready")
        p3T_done = sem("p3T_done")
        p3T_ready = sem("p3T_ready")
        vw_done = sem("vw_done")
        vw_ready = sem("vw_ready")
        cq_loaded = [sem("cq_loaded0"), sem("cq_loaded1")]
        qn_loaded = [sem("qn_loaded0"), sem("qn_loaded1")]
        xr_loaded = [sem("xr_loaded0"), sem("xr_loaded1")]
        qT_done = sem("qT_done")
        qT_ready = sem("qT_ready")
        out_done = sem("out_done")
        res_ready = sem("res_ready")
        stored = [sem("stored0"), sem("stored1")]

        block = ctx.enter_context(nc.Block())

        CQ = NB // 2

        def cq_bank(c):
            if c < 8:
                return (c // 2) % 2, c % 2
            return (0 if c < 10 else 1), c % 2

        def cq_before(c):
            return max((d + 1 for d in range(c) if cq_bank(d) == cq_bank(c)), default=0)

        def tokens(t, b):
            return t[bass.ds(b, 1), :, :].rearrange("o (p t) c -> (o p) t c", t=T)

        def up_weights(eng, w, name, g, done):
            eng.dma_start(w[:, g % RING, :, :], a[name][g * G:(g + 1) * G].rearrange("e c f -> c e f")).then_inc(done, DMA)

        def down_weights(eng, g, done):
            for j in range(G):
                eng.dma_start(W2[:, g % RING, j, :, :], a["L0_ffn_e_W2"][g * G + j].rearrange("(k p) c -> p k c", p=P))\
                   .then_inc(done, DMA)

        EXPERTS = 3 * RING * G * DMA
        FIRST1, LAST1, LO1, HI1 = -3, NB + 1, 4, NB - 4
        assert HI1 - LO1 == 2 * RING * G
        FIRST3, LAST3, LO3, HI3 = -1, NB + 1, 6, NB - 2

        @block.sync
        def _(sp):
            def load(dst, src, done):
                sp.dma_start(dst, src).then_inc(done, DMA)

            def load_x(b):
                sp.dma_start(xin[:, b.par, :, :], tokens(x, b.val())).then_inc(x_loaded[b.par], DMA)

            load_x(single(0))
            load(WB[:, 0:3 * C], a["L0_attn_qkv_w"], ld_fold)
            load(WB[:, 3 * C:4 * C], a["L0_ffn_d_Wv"], ld_fold)
            load(setup_bb[:, 0:3 * C], a["L0_attn_qkv_b"].partition_broadcast(P), ld_fold)
            load(setup_bb[:, 3 * C:], a["L0_ffn_d_bv"].partition_broadcast(P), ld_fold)
            load_x(single(1))
            load(pW[:, :], a["L0_attn_proj_w"], ld_pW)

            def column(i, name):
                return cols[:, i:i + 1], a[name].rearrange("(p o) -> p o", o=1), ld_rest

            def row(i, name):
                return rows[:, i * C:(i + 1) * C], a[name].rearrange("(o n) -> o n", o=1), ld_rest

            def pieces(lo, hi, name):
                return (bias_left[:, lo // BJ:hi // BJ], a[name].rearrange("e (j c) -> (e j) c", j=BJ), ld_bias)

            later = {
                0: (pieces(0, F, "L0_ffn_e_b1"), pieces(F, 2 * F, "L0_ffn_e_bg"),
                    pieces(2 * F, 2 * F + C, "L0_ffn_e_b2"),
                    (bias_left[:, (2 * F + C) // BJ:], a["L0_ffn_slot_query"][0].rearrange("e (j c) -> (e j) c", j=BJ),
                     ld_bias)),
                1: ((bias_dbo[:, :], a["L0_ffn_d_bo"].rearrange("(j c) -> j c", j=BJ).unsqueeze(0)
                     .to_broadcast([E, BJ, C // BJ]), ld_bias),
                    (gb16[:, 0, :], a["L0_ffn_e_ln_g"], ld_rest), (gb16[:, 1, :], a["L0_ffn_e_ln_b"], ld_rest),
                    (dWo[:, :], a["L0_ffn_d_Wo"], ld_rest)),
                2: ((cWk[:, :], a["L0_ffn_c_Wk"], ld_rest), (cWv[:, :], a["L0_ffn_c_Wv"], ld_rest),
                    (cWo[:, :], a["L0_ffn_c_Wo"], ld_rest), (WB[:, 4 * C:5 * C], a["L0_ffn_c_Wq"], ld_rest)),
                3: (column(2, "L0_ffn_c_bk"), column(3, "L0_ffn_c_bv"), row(0, "L0_ffn_c_bq"),
                    row(1, "L0_attn_proj_b"), row(2, "L0_ffn_c_bo")),
            }

            def step(i):
                b = i.at(-1)
                if b.ok(NB):
                    sp.wait_ge(qk_ready, b.count())
                    sp.dma_start(qn_all[:, bass.ds(b.val(), 1), :, :], qk[:, b.par:b.par + 1, :, 0:C])\
                      .then_inc(q_saved[b.par], DMA)
                b = i.at(4)
                if b.ok(NB) and (b.inside or b.val() >= 2):
                    sp.wait_ge(xm_ready, b.count(-2))
                    load_x(b)
                b = i.at(1)
                if b.ok(NB):
                    sp.wait_ge(xT_ready, b.count())
                    sp.dma_start(xnT_all[:, bass.ds(b.val(), 1), :], xnT[:, b.par:b.par + 1, :])\
                      .then_inc(xT_saved[b.par], DMA)
                if i.inside and i.off == 0:
                    n = i.base - LO1
                    load(W1[:, :, :, :].rearrange("p r g f -> p (r g f)")[:, bass.ds(n * (F // 2), F)],
                         a["L0_ffn_e_W1"].rearrange("e c f -> (e c) f")[bass.ds(n * (C // 2), C), :], ld_exp)
                    load(Wg[:, :, :, :].rearrange("p r g f -> p (r g f)")[:, bass.ds(n * (F // 2), F)],
                         a["L0_ffn_e_Wg"].rearrange("e c f -> (e c) f")[bass.ds(n * (C // 2), C), :], ld_exp)
                    load(W2[:, :, :, :, :].rearrange("p r g k c -> p (r g k) c")[:, bass.ds(n * (FK // 2), FK), :],
                         a["L0_ffn_e_W2"].rearrange("e f c -> (e f) c")[bass.ds(n * (F // 2), F), :]
                         .rearrange("(k p) c -> p k c", p=P), ld_exp)
                for k, loads in later.items():
                    if i.now(k):
                        for dst, src, done in loads:
                            load(dst, src, done)
                if i.now(NB - 3):
                    sp.wait_ge(sel_const, 1)
                    for k in range(1, 3):
                        load(sel[k * E:(k + 1) * E, :, :], sel[0:E, :, :], bias_moved)
                if i.now(NB - 2):
                    sp.wait_ge(split_act, 3)
                    for k in range(3):
                        load(bias3[k * E:(k + 1) * E, :].rearrange("e (j c) -> e j c", j=BJ), bias_part[:, k, :],
                             bias_moved)

            run_steps(sp, step, FIRST1 - 1, LAST1, LO1, HI1)
            for g in range(RING, NG):
                sp.wait_ge(e_u_done, g - RING + 1)
                up_weights(sp, W1, "L0_ffn_e_W1", g, ld_W1)
                sp.wait_ge(e_g_done, g - RING + 1)
                up_weights(sp, Wg, "L0_ffn_e_Wg", g, ld_Wg)
                sp.wait_ge(e_y_done, g - RING + 1)
                down_weights(sp, g, ld_W2)

            def step3(i):
                b = i.at(2)
                if b.ok(NB):
                    if not i.inside:
                        sp.wait_ge(cq_ready, CQ if i.now(LO3 - 1) else b.val() // 2 + 1)
                    if b.inside or b.val() >= 2:
                        sp.wait_ge(s3_done, b.count(-2))
                    sp.dma_start(cqT[:, b.par:b.par + 1, :], xnT_all[:, bass.ds(b.val(), 1), :])\
                      .then_inc(cq_loaded[b.par], DMA)
                b = i.at(1)
                if b.ok(NB):
                    if b.inside or b.val() >= 2:
                        sp.wait_ge(qT_done, b.count(-2))
                    sp.dma_start(qns[:, b.par, :, :],
                                 qn_all[:, :, :, :].rearrange("p b t c -> p (b t) c")[:, bass.ds(b.val() * T, T), :])\
                      .then_inc(qn_loaded[b.par], DMA)
                b = i.at(-3)
                if b.ok(NB):
                    sp.wait_ge(res_ready, b.count())
                    sp.dma_start(tokens(out, b.val()), res[:, b.par, :, :]).then_inc(stored[b.par], DMA)
                b = i.at(-1)
                if b.ok(NB):
                    if b.inside or b.val() >= 2:
                        sp.wait_ge(res_ready, b.count(-2))
                    sp.dma_start(xr[:, b.par, :, :], tokens(x, b.val())).then_inc(xr_loaded[b.par], DMA)

            for r in range(2):
                sp.wait_ge(q_saved[r], DMA * NB // 2)
            sp.wait_ge(e_g_done, NG)
            run_steps(sp, step3, -2, LAST3 + 1, LO3, HI3)
            for r in range(2):
                sp.wait_ge(stored[r], DMA * NB // 2)

        @block.gpsimd
        def _(pool):
            def select(out_, compare, base, pattern, channel):
                return pool.affine_select(out=out_, in_=out_, compare_op=compare, fill=0.0, base=base,
                                          pattern=pattern, channel_multiplier=channel)

            pool.memset(ident[:, :], 1.0)
            pool.memset(mask16[:, :], 1.0)
            pool.memset(neg[:, :], -1.0 / C)
            pool.memset(pos[:, :], 1.0 / C)
            pool.memset(one[:, :], 1.0)
            pool.memset(lnshift[:, :], 0.5 * LN_SHIFT * math.log(2.0)).then_inc(pool_const, 1)
            pool.wait_ge(pool_const, 1)
            select(ident[:, :], ALU.is_equal, 0, [[-1, P]], 1).then_inc(ident_const, 1)
            select(mask16[:, :], ALU.is_ge, 0, [[-D, H]], 1).then_inc(pool_const, 1)
            pool.wait_ge(pool_const, 2)
            select(mask16[:, :], ALU.is_ge, D - 1, [[D, H]], -1).then_inc(pool_const, 1)

            def step(i):
                b = i.at(2)
                if b.ok(NB):
                    p = b.par
                    pool.wait_ge(rinv_ready, b.count())
                    pool.wait_ge(mv_done, b.count())
                    if b.inside or b.val() >= 2:
                        pool.wait_ge(xT_done, b.count(-2))
                    pool.tensor_tensor(xn[:, p, :, :], xin[:, p, :, :], mv[:, p, :, 0:1].to_broadcast([P, T, C]),
                                       ALU.subtract).then_inc(xm_ready, 1)
                    pool.wait_ge(xm_ready, b.count())
                    pool.tensor_tensor(xn[:, p, :, :], xn[:, p, :, :],
                                       rinv[:, 1 - p, NR:NR + T].unsqueeze(2).to_broadcast([P, T, C]), ALU.mult)\
                        .then_inc(xn_ready, 1)
                b = i.at(-1)
                if b.ok(NB):
                    p = b.par
                    pool.wait_ge(rsum_ready, b.count())
                    v = pr[:, p, :].rearrange("p (k n) -> p k n", k=HC)
                    pool.tensor_tensor(v, v, rsum[:, p, :].unsqueeze(2).to_broadcast([P, HC, N]), ALU.mult)\
                        .then_inc(p_ready, 1)
                if i.now(1):
                    pool.memset(sel[0:E, :, :], 1.0).then_inc(pool_const, 1)
                    pool.wait_ge(pool_const, 4)
                    select(sel[0:E, :, :], ALU.is_equal, 0, [[-1, E], [0, NB]], 1).then_inc(sel_const, 1)
                if i.now(2):
                    query = bias_left[:, (2 * F + C) // BJ:]
                    pool.wait_ge(ld_bias, BIAS_DMAS * DMA)
                    pool.tensor_tensor(query, query, bias_dbo[:, :], ALU.add).then_inc(split_pool, 1)
                for k in range(2):
                    if i.now((3, HI1)[k]):
                        pool.wait_ge(split_act, k + 1)
                        pool.tensor_tensor(bias_left[:, :], bias_left[:, :], bias_part[:, k, :], ALU.subtract)\
                            .then_inc(split_pool, 1)

            run_steps(pool, step, FIRST1, LAST1, LO1, HI1)

            heads = mask16[:, :].unsqueeze(2).to_broadcast([P, H, E])

            def step3(i):
                b = i.at(-1)
                if b.ok(NB):
                    p = b.par
                    pool.wait_ge(rden_ready, b.count())
                    v = pr[:, p, :].rearrange("p (h e) -> p h e", e=E)
                    pool.tensor_tensor(v, v, rden[:, p, :].unsqueeze(2).to_broadcast([P, T * H, E]), ALU.mult)\
                        .then_inc(p3_ready, 1)
                for b, blk, src, used, ready in ((i.at(0), vblk, vT, vw_done, vblk_ready),
                                                 (i.at(2), kblk, kT, s3_done, kblk_ready)):
                    if b.ok(NB):
                        if b.inside or b.val() >= 2:
                            pool.wait_ge(used, b.count(-2))
                        sl = src[:, :, bass.ds(b.val(), 1)].rearrange("p e o -> p o e").to_broadcast([P, H, E])
                        pool.tensor_tensor(blk[:, b.par, :].rearrange("p (h e) -> p h e", h=H), sl, heads, ALU.mult)\
                            .then_inc(ready, 1)

            pool.wait_ge(e_kv_ready, 3)
            step3(single(-2))
            step3(single(-1))
            pool.wait_ge(e_kv_ready, 4)
            run_steps(pool, step3, 0, LAST3, LO3, HI3)

        @block.scalar
        def _(act):
            act.preload_act_table_set("natural_log_exp_and_others")
            for dst, src in ((setup_wk, a["L0_ffn_d_Wk"]), (sq16[:, :], a["L0_ffn_slot_query"][0]),
                             (setup_wq, a["L0_ffn_d_Wq"]),
                             (cols[:, 0:1], a["L0_ffn_d_bq"].rearrange("(p o) -> p o", o=1)),
                             (cols[:, 1:2], a["L0_ffn_d_bk"].rearrange("(p o) -> p o", o=1))):
                act.dma_start(dst, src).then_inc(ld_slot, DMA)
            act.wait_ge(pool_const, 1)

            def queries(c):
                act.wait_ge(cq_done, c + 1)
                act.activation(xnT_all[:, 2 * c:2 * c + 2, :].rearrange("p b n -> p (b n)"), psB[:, cq_bank(c)[0], cq_bank(c)[1], :],
                               ACT.Copy).then_inc(cq_ready, 1)

            def step(i):
                b = i.at(0)
                if b.ok(NB):
                    p = b.par
                    act.wait_ge(qkv_done, b.count())
                    if b.inside or b.val() >= 1:
                        act.wait_ge(ssum_done, b.count(-1))
                    act.activation(sq[:, :, :], psB[:, p, :, 0:2 * C], ACT.Square).then_inc(sq_ready, 1)
                b = i.at(1)
                if b.ok(NB):
                    p = b.par
                    act.wait_ge(xT_done, b.count())
                    if b.inside or b.val() >= 2:
                        act.wait_ge(scores_done, b.count(-2))
                        act.wait_ge(xT_saved[p], b.dmas(-2))
                    if i.at(-2).ok(NB):
                        act.wait_ge(m_done, i.count(-2))
                    act.activation(xnT[:, p, :], psX[:, 0:N], ACT.Copy, bias=1.0).then_inc(xT_ready, 1)
                b = i.at(-2)
                if b.ok(NB):
                    act.wait_ge(m_done, b.count())
                    act.activation(M_all[:, bass.ds(b.val(), 1), :], psX[:, N:N + C].unsqueeze(1), ACT.Copy)\
                       .then_inc(m_ready, 1)
                b = i.at(0)
                if b.ok(NB):
                    p = b.par
                    if b.inside or b.val() >= 2:
                        act.wait_ge(slot_done, b.count(-2))
                    act.activation(vv[:, p, :, :], psB[:, p, :, 2 * C:4 * C], ACT.Copy).then_inc(v_ready, 1)
                lo = 0 if i.ok(NB) else NR
                hi = NR + T if i.at(3).ok(NB) else NR
                if lo < hi:
                    p = i.par
                    if i.ok(NB):
                        act.wait_ge(ss_ready, i.count())
                    if i.at(3).ok(NB):
                        act.wait_ge(var_ready, i.count(3))
                    act.activation(lnb[:, lo:hi], small[:, p, lo:hi], ACT.Ln,
                                   scale=-2.0 ** (LN_SHIFT + 1))\
                       .then_inc(ln_done, 1)
                    act.wait_ge(ln_done, i.count(3))
                    act.activation(rinv0[:, p, lo:hi], lnb[:, lo:hi], ACT.Exp, scale=-0.5,
                                   bias=lnshift[:, 0:1]).then_inc(rinv0_ready, 1)
                b = i.at(-1)
                if b.ok(NB):
                    p = b.par
                    act.wait_ge(pT_done, b.count())
                    if b.inside or b.val() >= 2:
                        act.wait_ge(slot_done, b.count(-2))
                    act.activation(prT[:, p, :], psT[:, :], ACT.Copy).then_inc(pT_ready, 1)
                b = i.at(0)
                if b.ok(NB):
                    p = b.par
                    act.wait_ge(max_ready, b.count())
                    if b.inside or b.val() >= 2:
                        act.wait_ge(pT_done, b.count(-2))
                    for k in range(HC):
                        last = act.activation(pr[:, p, k * N:(k + 1) * N], psS[:, k * N:(k + 1) * N], ACT.Exp,
                                              bias=nmax[:, p, k:k + 1], accum_out=ssum[:, p, k:k + 1])
                    last.then_inc(exp_ready, 1)
                for k in range(3):
                    if i.now((3, HI1, HI1 + 1)[k]):
                        act.wait_ge(split_pool, k + 1)
                        act.activation(bias_part[:, k, :], bias_left[:, :], ACT.Copy).then_inc(split_act, 1)

                if i.now(NB) or i.now(NB + 1):
                    queries(i.base + i.off - NB)

            run_steps(act, step, FIRST1, LAST1, LO1, HI1)

            queries(2)
            for g in range(NG):
                act.wait_ge(e_o, g + 1)
                act.activation(o_tm[:, g, :], slot_banks[g], ACT.Copy).then_inc(e_o_ready, 1)
            queries(3)
            act.wait_ge(e_var_ready, 1)
            act.activation(lnb[:, 0:NG], small[:, 0, 0:NG], ACT.Ln, scale=-2.0).then_inc(e_ln_done, 1)
            act.wait_ge(e_ln_done, 1)
            act.activation(rinv0[:, 0, 0:NG], lnb[:, 0:NG], ACT.Exp, scale=-0.5).then_inc(e_rinv0_ready, 1)
            act.preload_act_table(ACT.Silu)
            for c in range(4, 8):
                queries(c)
            for r in range(2):
                act.wait_ge(q_saved[r], DMA * NB // 2)

            def silu(g):
                if g:
                    act.wait_ge(e_ug_ready, g)
                act.wait_ge(e_u_done, g + 1)
                act.activation(silu_u, psU[:, g % 2, :], ACT.Silu)
                act.wait_ge(e_g_done, g + 1)
                act.activation(silu_g, psG[:, g % 2, :], ACT.Silu).then_inc(e_silu_ready, 1)

            silu(0)
            for g in range(NG):
                if g + 1 < NG:
                    silu(g + 1)
                act.wait_ge(e_ugT_done, g + 1)
                if g:
                    act.wait_ge(e_y_done, g)
                act.activation(ugT, psT[:, :], ACT.Copy).then_inc(e_ugT_ready, 1)
                if g == NG - 2:
                    queries(8)
                    queries(9)
            queries(10)
            act.wait_ge(e_oT_done, 1)
            act.activation(oT[:, 0:(NG - 1) * C], psX[:, 0:(NG - 1) * C], ACT.Copy).then_inc(e_oT_ready, 1)
            queries(11)
            act.preload_act_table_set("natural_log_exp_and_others")
            act.wait_ge(e_oT_done, 2)
            act.activation(oT[:, (NG - 1) * C:], psX[:, (NG - 1) * C:], ACT.Copy).then_inc(e_oT_ready, 1)
            for c in range(12, CQ):
                queries(c)

            def step3(i):
                b = i.at(-1)
                if b.ok(NB):
                    p = b.par
                    act.wait_ge(qT_done, b.count())
                    if b.inside or b.val() >= 2:
                        act.wait_ge(out_done, b.count(-2))
                    act.activation(qT[:, p, :], psK[:, 0:N], ACT.Copy).then_inc(qT_ready, 1)
                b = i.at(0)
                if b.ok(NB):
                    act.wait_ge(sub_ready, b.count())
                    act.activation(pr[:, b.par, :], pr[:, b.par, :], ACT.Exp, scale=SC).then_inc(exp3_ready, 1)
                b = i.at(-1)
                if b.ok(NB):
                    act.wait_ge(p3T_done, b.count())
                    if b.inside or b.val() >= 2:
                        act.wait_ge(out_done, b.count(-2))
                    act.activation(prT[:, b.par, :], psT[:, :], ACT.Copy).then_inc(p3T_ready, 1)

            run_steps(act, step3, 0, LAST3, LO3, HI3)

        @block.vector
        def _(dve):
            dve.wait_ge(pool_const, 3)
            dve.tensor_copy(bmask[:, :].rearrange("p (h d) -> p h d", h=H),
                            mask16[:, :].unsqueeze(2).to_broadcast([P, H, D])).then_inc(dve_const, 1)
            dve.tensor_reduce(mask4[:, :], mask16[:, :].rearrange("p (j h) -> p h j", h=G), AX_X, ALU.add)\
               .then_inc(dve_const, 1)
            def step(i):
                b = i.at(3)
                if b.ok(NB):
                    p = b.par
                    dve.wait_ge(x_loaded[p], b.dmas())
                    for t in range(T):
                        last = dve.bn_stats(bnst[:, p, t, :], xin[:, p, t, :])
                    last.then_inc(bn_done, 1)
                    dve.wait_ge(bn_done, b.count())
                b = i.at(-1)
                if b.ok(NB):
                    p = b.par
                    dve.wait_ge(rinv_ready, b.count(3))
                    dve.wait_ge(v_ready, b.count())
                    if b.inside or b.val() >= 2:
                        dve.wait_ge(kv_done, b.count(-2))
                        dve.wait_ge(q_saved[p], b.dmas(-2))
                    for t in range(T):
                        last = dve.tensor_tensor(
                            qk[:, p, t, :].rearrange("p (h d) -> p h d", d=D),
                            psB[:, p, t, 0:2 * C].rearrange("p (h d) -> p h d", d=D),
                            rinv[:, p, t * 2 * H:(t + 1) * 2 * H].unsqueeze(2).to_broadcast([P, 2 * H, D]), ALU.mult)
                    last.then_inc(qk_ready, 1)
                b = i.at(-1)
                if b.ok(NB):
                    dve.wait_ge(exp_ready, b.count())
                    dve.reciprocal(rsum[:, b.par, :], ssum[:, b.par, :]).then_inc(rsum_ready, 1)
                b = i.at(3)
                if b.ok(NB):
                    p = b.par
                    for t in range(T):
                        last = dve.bn_aggr(mv[:, p, t, :], bnst[:, p, t, :])
                    last.then_inc(mv_done, 1)
                if i.now(NB):
                    dve.wait_ge(late_done, 1)
                    dve.tensor_tensor(WB[:, 4 * C:5 * C], WB[:, 4 * C:5 * C], psU[:, 0, 0:C], ALU.add)
                    dve.tensor_scalar(outb[:, :], psU[:, 0, C:2 * C], 1.0 / H, None, ALU.mult)
                    dve.tensor_copy(gbT[:, :, :], psU[:, 0, 2 * C:2 * C + 2 * E].rearrange("p (k e) -> p k e", k=2))\
                       .then_inc(late_ready, 1)
                b = i.at(0)
                if b.ok(NB):
                    dve.wait_ge(sq_ready, b.count())
                    if b.inside or b.val() >= 1:
                        dve.wait_ge(ss_ready, b.count(-1))
                    dve.tensor_reduce(ssq[:, :], sq[:, :, :].rearrange("p t (h d) -> p (t h) d", d=D), AX_X,
                                      ALU.add).then_inc(ssum_done, 1)
                b = i.at(3)
                if b.ok(NB):
                    dve.wait_ge(mv_done, b.count())
                    dve.tensor_scalar(small[:, i.par, NR:NR + T], mv[:, b.par, :, 1], LN_EPS, -0.5,
                                      ALU.add, ALU.mult)\
                       .then_inc(var_ready, 1)
                b = i.at(0)
                if b.ok(NB):
                    dve.wait_ge(ssum_done, b.count())
                    dve.tensor_scalar(small[:, b.par, 0:NR], ssq[:, :], L2_GUARD, -0.5, ALU.max, ALU.mult)\
                       .then_inc(ss_ready, 1)
                b = i.at(-2)
                if b.ok(NB):
                    dve.wait_ge(slot_done, b.count())
                    if b.inside or b.val() >= 1:
                        dve.wait_ge(slot_ready, b.count(-1))
                    dve.tensor_tensor(rm[:, :, :], psC[:, C:C + G * E].rearrange("p (h e) -> p h e", h=G),
                                      mask4[:, :].unsqueeze(2).to_broadcast([P, G, E]), ALU.mult)\
                       .then_inc(slot_masked, 1)
                b = i.at(0)
                if b.ok(NB):
                    dve.wait_ge(scores_done, b.count())
                    dve.tensor_reduce(nmax[:, b.par, :], psS[:, :].rearrange("p (k n) -> p k n", k=HC), AX_X,
                                      ALU.max, negate=True).then_inc(max_ready, 1)
                lo = 0 if i.ok(NB) else NR
                hi = NR + T if i.at(3).ok(NB) else NR
                y = rinv0[:, i.par, lo:hi]
                if lo < hi:
                    dve.wait_ge(rinv0_ready, i.count(3))
                    dve.tensor_tensor(nwt[:, 0, lo:hi], y, y, ALU.mult).then_inc(newton1, 1)
                b = i.at(-2)
                if b.ok(NB):
                    dve.wait_ge(slot_masked, b.count())
                    dve.tensor_reduce(slots[:, :, bass.ds(b.val(), 1)],
                                      rm[:, :, :].rearrange("p h e -> p e h"), AX_X, ALU.add).then_inc(slot_ready, 1)
                if lo < hi:
                    dve.wait_ge(newton1, i.count(3))
                    dve.tensor_tensor(nwt[:, 1, lo:hi], nwt[:, 0, lo:hi], small[:, i.par, lo:hi], ALU.mult)\
                       .then_inc(newton2, 1)
                b = i.at(-1)
                if b.ok(NB):
                    dve.wait_ge(kv_done, b.count())
                    dve.tensor_tensor(kvm[:, b.par, :], psC[:, 0:C], bmask[:, :], ALU.mult).then_inc(kvm_ready, 1)
                if lo < hi:
                    dve.wait_ge(newton2, i.count(3))
                    dve.scalar_tensor_tensor(rinv[:, i.par, lo:hi], nwt[:, 1, lo:hi], 1.5, y, ALU.add, ALU.mult)\
                       .then_inc(rinv_ready, 1)

            step(single(-3))
            dve.wait_ge(ld_fold, FOLD_DMAS * DMA)
            dve.scalar_tensor_tensor(setup_bb, setup_bb, 1.0 / C, WB[:, 0:4 * C], ALU.mult, ALU.add)\
               .then_inc(dve_setup, 1)
            dve.wait_ge(pe_setup, 1)
            dve.wait_ge(dve_setup, 1)
            dve.tensor_tensor(WB[:, 0:4 * C], setup_bb, psU[:, 0, :], ALU.add).then_inc(dve_setup, 1)
            dve.wait_ge(pe_setup, 2)
            dve.tensor_copy(setup_sqT, psC[:, C:C + E]).then_inc(dve_setup, 1)
            dve.tensor_copy(setup_wkT, psC[:, 0:C])
            dve.wait_ge(ld_slot, SLOT_DMAS * DMA)
            dve.memset(setup_bk, 1.0 / C).then_inc(dve_setup, 1)
            dve.wait_ge(dve_setup, 4)
            dve.tensor_scalar(setup_bk, setup_bk, cols[:, 1:2], None, ALU.mult).then_inc(dve_setup, 1)
            step(single(-2))
            dve.wait_ge(pe_setup, 3)
            dve.tensor_scalar(setup_q, psS[:, HS:HS + E], cols[:, 0:1], SC, ALU.add, ALU.mult).then_inc(dve_setup, 1)
            dve.wait_ge(dve_setup, 6)
            dve.tensor_tensor(setup_qblk.rearrange("p (h e) -> p h e", h=H),
                              setup_q.unsqueeze(1).to_broadcast([P, H, E]),
                              mask16[:, :].unsqueeze(2).to_broadcast([P, H, E]), ALU.mult).then_inc(dve_setup, 1)
            dve.wait_ge(pe_setup, 4)
            dve.tensor_copy(Wslot[:, :], psS[:, 0:HS]).then_inc(dve_setup, 1)
            step(single(-1))
            dve.wait_ge(pe_setup, 5)
            dve.tensor_tensor(Wslot[:, :], Wslot[:, :], psT[:, 0:HS], ALU.add).then_inc(dve_setup, 1)
            run_steps(dve, step, 0, LAST1, LO1, HI1)

            for g in range(NG):
                dve.wait_ge(e_o_ready, g + 1)
                last = dve.bn_stats(bnst[:, g // 2, g % 2, :], o_tm[:, g, :])
            last.then_inc(bn_done, 1)
            dve.wait_ge(bn_done, NB + 1)
            for g in range(NG):
                last = dve.bn_aggr(mv[:, g // 2, g % 2, :], bnst[:, g // 2, g % 2, :])
            last.then_inc(mv_done, 1)
            dve.wait_ge(mv_done, NB + 1)
            half_v, y0 = small[:, 0, 0:NG], rinv0[:, 0, 0:NG]
            dve.tensor_scalar(half_v, mv[:, :, :, 1].rearrange("p a t -> p (a t)"), LN_EPS, -0.5, ALU.add, ALU.mult)\
               .then_inc(e_var_ready, 1)
            dve.wait_ge(e_rinv0_ready, 1)
            dve.tensor_tensor(nwt[:, 0, 0:NG], y0, half_v, ALU.mult).then_inc(e_newton, 1)
            dve.wait_ge(e_newton, 1)
            dve.tensor_tensor(nwt[:, 1, 0:NG], nwt[:, 0, 0:NG], y0, ALU.mult).then_inc(e_newton, 1)
            dve.wait_ge(e_newton, 2)
            dve.scalar_tensor_tensor(rinv[:, 0, 0:NG], nwt[:, 1, 0:NG], 1.5, y0, ALU.add, ALU.mult)\
               .then_inc(e_newton, 1)
            dve.wait_ge(e_newton, 3)
            for g in range(NG):
                dve.tensor_scalar(hn[:, g, :], o_tm[:, g, :], mv[:, g // 2, g % 2, 0:1], rinv[:, 0, g:g + 1],
                                  ALU.subtract, ALU.mult).then_inc(e_hn_ready, 1)
            h3 = hT.rearrange("p (e b) -> p e b", e=E)
            for g in range(NG):
                eg = slice(g * G, (g + 1) * G)
                dve.wait_ge(e_hnT_done, g + 1)
                dve.tensor_tensor(h3[:, eg, :], slot_banks[g].rearrange("p (e b) -> p e b", e=G), gbT[:, 0, eg].unsqueeze(2).to_broadcast([P, G, NB]),
                                  ALU.mult).then_inc(e_hg_done, 1)
                dve.wait_ge(e_hg_done, g + 1)
                dve.tensor_tensor(h3[:, eg, :], h3[:, eg, :], gbT[:, 1, eg].unsqueeze(2).to_broadcast([P, G, NB]),
                                  ALU.add).then_inc(e_h_ready, 1)
            for g in range(NG):
                dve.wait_ge(e_silu_ready, g + 1)
                if g:
                    dve.wait_ge(e_ugT_done, g)
                dve.tensor_tensor(ug, silu_u, silu_g, ALU.mult).then_inc(e_ug_ready, 1)
                if g:
                    dve.wait_ge(e_y_done, g)
                    dve.tensor_tensor(o2_tm[:, g - 1, :], psY[:, 0:C], o_tm[:, g - 1, :], ALU.add)\
                       .then_inc(e_o2_ready, 1)
            dve.wait_ge(e_y_done, NG)
            dve.tensor_tensor(o2_tm[:, NG - 1, :], psY[:, 0:C], o_tm[:, NG - 1, :], ALU.add).then_inc(e_o2_ready, 1)
            n = 0
            for g, keys, values in kv_parts:
                cols_ = slice(g * C, E * NB if g else (NG - 1) * C)
                width = cols_.stop - cols_.start
                for dst, src, k in ((kT, keys, 2), (vT, values, 3)):
                    n += 1
                    dve.wait_ge(e_kv_done, n)
                    dve.tensor_scalar(dst[:, :, :].rearrange("p e b -> p (e b)")[:, cols_], src[:, 0:width],
                                      cols[:, k:k + 1], None, ALU.add).then_inc(e_kv_ready, 1)

            def step3(i):
                s3 = psS[:, :].rearrange("p (h e) -> p h e", e=E)
                b = i.at(0)
                if b.ok(NB):
                    p = b.par
                    dve.wait_ge(s3_done, b.count())
                    dve.tensor_reduce(top, s3, AX_X, ALU.max).then_inc(top_ready, 1)
                b = i.at(-1)
                if b.ok(NB):
                    p = b.par
                    dve.wait_ge(vw_done, b.count())
                    if b.inside or b.val() >= 2:
                        dve.wait_ge(out_done, b.count(-2))
                    dve.tensor_tensor(vw[:, p, :, :], psV[:, 0:N].rearrange("p (k c) -> p k c", k=HC),
                                      outb[:, :].unsqueeze(1).to_broadcast([P, HC, C]), ALU.add).then_inc(vw_ready, 1)
                b = i.at(0)
                if b.ok(NB):
                    p = b.par
                    dve.wait_ge(top_ready, b.count())
                    if b.inside or b.val() >= 2:
                        dve.wait_ge(p3T_done, b.count(-2))
                    dve.tensor_tensor(pr[:, p, :].rearrange("p (h e) -> p h e", e=E), s3,
                                      top.unsqueeze(2).to_broadcast([P, T * H, E]), ALU.subtract)\
                       .then_inc(sub_ready, 1)
                b = i.at(-3)
                if b.ok(NB):
                    p = b.par
                    dve.wait_ge(out_done, b.count())
                    dve.wait_ge(xr_loaded[p], b.dmas())
                    if b.inside or b.val() >= 2:
                        dve.wait_ge(stored[p], b.dmas(-2))
                    dve.tensor_tensor(res[:, p, :, :], psO[:, p, 0:N].rearrange("p (t c) -> p t c", t=T),
                                      xr[:, p, :, :], ALU.add).then_inc(res_ready, 1)
                b = i.at(0)
                if b.ok(NB):
                    p = b.par
                    dve.wait_ge(exp3_ready, b.count())
                    if b.inside or b.val() >= 1:
                        dve.wait_ge(rden_ready, b.count(-1))
                    dve.tensor_reduce(den, pr[:, p, :].rearrange("p (h e) -> p h e", e=E), AX_X, ALU.add)\
                       .then_inc(den_ready, 1)
                    dve.wait_ge(den_ready, b.count())
                    dve.reciprocal(rden[:, p, :], den).then_inc(rden_ready, 1)
            run_steps(dve, step3, 0, LAST3 + 1, LO3, HI3)

        @block.tensor
        def _(pe):
            pe.wait_ge(pool_const, 1)
            pe.wait_ge(ld_fold, FOLD_DMAS * DMA)
            pe.matmul(psU[:, 0, :], neg[:, :], WB[:, 0:4 * C], start=True, stop=True).then_inc(pe_setup, 1)
            pe.wait_ge(ident_const, 1)
            pe.wait_ge(ld_slot, SLOT_DMAS * DMA)
            pe.transpose(psC[:, 0:C], setup_wk, ident[:, :])
            pe.transpose(psC[:, C:C + E], sq16[:, :], ident[0:E, 0:E]).then_inc(pe_setup, 1)
            pe.wait_ge(dve_setup, 3)
            pe.matmul(psS[:, HS:HS + E], setup_wq, setup_sqT, start=True, stop=True).then_inc(pe_setup, 1)
            def queries(c):
                if c == 0:
                    for r in range(2):
                        pe.wait_ge(xT_saved[r], DMA * NB // 2)
                    pe.wait_ge(late_ready, 1)
                elif c == 2:
                    pe.wait_ge(qk_ready, NB)
                elif c >= 8:
                    pe.wait_ge(e_silu_ready, 3 if c < 10 else 4)
                if cq_before(c):
                    pe.wait_ge(cq_ready, cq_before(c))
                pe.matmul(psB[:, cq_bank(c)[0], cq_bank(c)[1], :], WB[:, 4 * C:5 * C],
                          xnT_all[:, 2 * c:2 * c + 2, :].rearrange("p b n -> p (b n)"),
                          start=True, stop=True).then_inc(cq_done, 1)

            def step(i):
                def project(t):
                    b = i.at(0)
                    p = b.par
                    if t == 0:
                        pe.wait_ge(xT_ready, b.count())
                        if b.inside or b.val() >= 2:
                            pe.wait_ge(qk_ready, b.count(-2))
                    return pe.matmul(psB[:, p, t, :], xnT[:, p, t * P:(t + 1) * P], WB[:, 0:4 * C],
                                     start=True, stop=True)

                if i.now(NB):
                    pe.wait_ge(ld_rest, REST_DMAS * DMA)
                    pe.wait_ge(qk_ready, NB - 1)
                    pe.matmul(psU[:, 0, 0:C], neg[:, :], WB[:, 4 * C:5 * C], start=True, stop=False)
                    pe.matmul(psU[:, 0, 0:C], pos[:, :], rows[:, 0:C], start=False, stop=True)
                    for k in range(2):
                        pe.matmul(psU[:, 0, C:2 * C], one[:, :], rows[:, (k + 1) * C:(k + 2) * C], start=(k == 0), stop=(k == 1))
                    for k in range(2):
                        last = pe.transpose(psU[:, 0, 2 * C + k * E:2 * C + (k + 1) * E], gb16[:, k, :], ident[0:E, 0:E])
                    last.then_inc(late_done, 1)
                if i.ok(NB):
                    project(0)
                    if i.now(0):
                        pe.wait_ge(dve_setup, 8)
                        pe.matmul(psT[:, 0:HS], neg[:, :], Wslot[:, :], start=True, stop=False)
                        pe.matmul(psT[:, 0:HS], setup_bk, setup_qblk, start=False, stop=True).then_inc(pe_setup, 1)
                    project(1).then_inc(qkv_done, 1)
                b = i.at(1)
                if b.ok(NB):
                    p = b.par
                    pe.wait_ge(xn_ready, b.count())
                    if b.inside or b.val() >= 1:
                        pe.wait_ge(xT_ready, b.count(-1))
                    if i.at(-3).ok(NB):
                        pe.wait_ge(m_ready, i.count(-3))
                    for t in range(T):
                        last = pe.transpose(psX[:, t * P:(t + 1) * P], xn[:, p, t, :], ident[:, :])
                    last.then_inc(xT_done, 1)
                b = i.at(-2)

                def project_kv():
                    if i.now(2):
                        pe.wait_ge(ld_pW, DMA)
                    pe.wait_ge(kvm_ready, b.count())
                    if b.inside or b.val() >= 1:
                        pe.wait_ge(m_ready, b.count(-1))
                    pe.matmul(psX[:, N:N + C], kvm[:, b.par, :], pW[:, :], start=True, stop=True).then_inc(m_done, 1)

                if b.ok(NB):
                    p = b.par
                    if not i.now(LAST1):
                        project_kv()
                    pe.wait_ge(kvm_ready, b.count())
                    pe.wait_ge(pT_ready, b.count())
                    for j in range(4):
                        for t in range(T):
                            last = pe.matmul(psC[32 * j:32 * j + 32, C:C + G * E],
                                             vv[:, p, t, C + 32 * j:C + 32 * j + 32],
                                             prT[:, p, t * HS + j * G * E:t * HS + (j + 1) * G * E],
                                             start=(t == 0), stop=(t == T - 1))
                    last.then_inc(slot_done, 1)
                    if i.now(LAST1):
                        project_kv()
                if i.now(NB):
                    queries(0)
                b = i.at(0)
                if b.ok(NB):
                    if i.now(0):
                        pe.wait_ge(dve_setup, 9)
                    if b.inside or b.val() >= 1:
                        pe.wait_ge(exp_ready, b.count(-1))
                    for k in range(HC):
                        last = pe.matmul(psS[:, k * N:(k + 1) * N], Wslot[:, k * P:(k + 1) * P], xnT[:, b.par, :],
                                         start=True, stop=True)
                    last.then_inc(scores_done, 1)
                b = i.at(-1)
                if b.ok(NB):
                    p = b.par
                    pe.wait_ge(p_ready, b.count())
                    if b.inside or b.val() >= 1:
                        pe.wait_ge(pT_ready, b.count(-1))
                    for t in range(T):
                        for k in range(HC):
                            last = pe.transpose(psT[:, t * HS + k * P:t * HS + (k + 1) * P],
                                                pr[:, p, k * N + t * P:k * N + (t + 1) * P], ident[:, :])
                    last.then_inc(pT_done, 1)
                    pe.wait_ge(qk_ready, b.count())
                    if b.inside or b.val() >= 1:
                        pe.wait_ge(slot_masked, b.count(-1))
                    for t in range(T):
                        last = pe.matmul(psC[:, 0:C], vv[:, p, t, 0:C], qk[:, p, t, C:2 * C],
                                         start=(t == 0), stop=(t == T - 1))
                    last.then_inc(kv_done, 1)
                if i.now(NB):
                    queries(1)

            step(single(-1))
            pe.wait_ge(dve_setup, 7)
            pe.matmul(psS[:, 0:HS], setup_wkT, setup_qblk, start=True, stop=True).then_inc(pe_setup, 1)
            run_steps(pe, step, 0, LAST1, LO1, HI1)

            def bias(dst, g, lo, n):
                pe.matmul(dst, sel[:, g * G:(g + 1) * G, :].rearrange("p e b -> p (e b)"),
                          bias3[:, :].rearrange("k (j c) -> k j c", j=BJ)[:, :, lo // BJ:(lo + n) // BJ],
                          start=True, stop=False, skip_group_check=True)

            queries(2)
            pe.wait_ge(slot_ready, NB)
            pe.wait_ge(m_ready, NB)
            pe.wait_ge(bias_moved, 5 * DMA)
            for g in range(NG):
                bias(slot_banks[g], g, 2 * F + C, C)
                pe.matmul(slot_banks[g], slots[:, g * G:(g + 1) * G, :].rearrange("p e b -> p (e b)"),
                          dWo[:, :], start=False, stop=True, skip_group_check=True).then_inc(e_o, 1)
            for c in range(3, 6):
                queries(c)
            for g in range(NG):
                pe.wait_ge(e_hn_ready, g + 1)
                pe.transpose(slot_banks[g], hn[:, g, :], ident[:, :]).then_inc(e_hnT_done, 1)
            queries(6)
            queries(7)
            pe.wait_ge(ld_exp, EXPERTS)
            pe.wait_ge(cq_ready, 8)

            def up(g, ps_, w, lo, loaded, done):
                pe.wait_ge(e_h_ready, g + 1)
                if g >= RING:
                    pe.wait_ge(loaded, (g - RING + 1) * DMA)
                if g >= 2:
                    pe.wait_ge(e_silu_ready, g - 1)
                dst = ps_[:, g % 2, :]
                bias(dst, g, lo, F)
                for j in range(G):
                    e = g * G + j
                    last = pe.matmul(dst[NB * j:NB * (j + 1), :], hT[:, e * NB:(e + 1) * NB], w[:, g % RING, j, :],
                                     start=False, stop=True, skip_group_check=True)
                last.then_inc(done, 1)

            def turn(g):
                pe.wait_ge(e_ug_ready, g + 1)
                if g:
                    pe.wait_ge(e_ugT_ready, g)
                for k in range(FK):
                    last = pe.transpose(psT[:, k * P:(k + 1) * P], ug[:, k * P:(k + 1) * P], ident[:, :])
                last.then_inc(e_ugT_done, 1)

            def down(g):
                pe.wait_ge(e_ugT_ready, g + 1)
                if g:
                    pe.wait_ge(e_o2_ready, g)
                if g >= RING:
                    pe.wait_ge(ld_W2, (g - RING + 1) * G * DMA)
                bias(psY[:, 0:C], g, 2 * F, C)
                for k in range(FK):
                    for j in range(G):
                        last = pe.matmul(psY[NB * j:NB * (j + 1), 0:C], ugT[:, k * P + NB * j:k * P + NB * (j + 1)],
                                         W2[:, g % RING, j, k, :], start=False, stop=(k == FK - 1),
                                         skip_group_check=True)
                last.then_inc(e_y_done, 1)

            for g in range(2):
                up(g, psU, W1, 0, ld_W1, e_u_done)
                up(g, psG, Wg, F, ld_Wg, e_g_done)
            def slots_turned(groups):
                for g in groups:
                    pe.wait_ge(e_o2_ready, g + 1)
                    last = pe.transpose(psX[:, g * C:(g + 1) * C], o2_tm[:, g, :], ident[:, :])
                last.then_inc(e_oT_done, 1)

            def slots_kv(part):
                g, keys, values = kv_parts[part]
                hi = E * NB if g else (NG - 1) * C
                pe.wait_ge(e_oT_ready, part + 1)
                for dst, w in ((keys, cWk), (values, cWv)):
                    pe.matmul(dst[:, 0:hi - g * C], w[:, :], oT[:, g * C:hi], start=True, stop=True).then_inc(e_kv_done, 1)

            for g in range(NG):
                turn(g)
                if g + 2 < NG:
                    up(g + 2, psU, W1, 0, ld_W1, e_u_done)
                if g == NG - 2:
                    queries(8)
                    queries(9)
                if g == NG - 1:
                    queries(10)
                    slots_turned(range(NG - 1))
                    queries(11)
                down(g)
                if g + 2 < NG:
                    up(g + 2, psG, Wg, F, ld_Wg, e_g_done)
            pe.wait_ge(cq_ready, 10)
            slots_kv(0)
            slots_turned((NG - 1,))
            queries(12)
            slots_kv(1)
            for c in range(13, CQ):
                queries(c)

            pe.wait_ge(e_kv_ready, 4)
            pe.wait_ge(cq_ready, CQ)

            def step3(i):
                b = i.at(0)
                if b.ok(NB):
                    p = b.par
                    pe.wait_ge(cq_loaded[p], b.dmas())
                    pe.wait_ge(kblk_ready, b.count())
                    if b.inside or b.val() >= 1:
                        pe.wait_ge(sub_ready, b.count(-1))
                    for t in range(T):
                        last = pe.matmul(psS[:, t * HS:(t + 1) * HS], cqT[:, p, t * P:(t + 1) * P], kblk[:, p, :],
                                         start=True, stop=True)
                    last.then_inc(s3_done, 1)
                b = i.at(-1)
                if b.ok(NB):
                    p = b.par
                    pe.wait_ge(vblk_ready, b.count())
                    if b.inside or b.val() >= 1:
                        pe.wait_ge(vw_ready, b.count(-1))
                    for k in range(HC):
                        last = pe.matmul(psV[:, k * C:(k + 1) * C], vblk[:, p, k * P:(k + 1) * P], cWo[:, :],
                                         start=True, stop=True)
                    last.then_inc(vw_done, 1)
                b = i.at(-1)
                if b.ok(NB):
                    p = b.par
                    pe.wait_ge(qn_loaded[p], b.dmas())
                    if b.inside or b.val() >= 1:
                        pe.wait_ge(qT_ready, b.count(-1))
                    for t in range(T):
                        last = pe.transpose(psK[:, t * P:(t + 1) * P], qns[:, p, t, :], ident[:, :])
                    last.then_inc(qT_done, 1)
                b = i.at(-2)
                if b.ok(NB):
                    p = b.par
                    pe.wait_ge(p3T_ready, b.count())
                    pe.wait_ge(vw_ready, b.count())
                    pe.wait_ge(qT_ready, b.count())
                    if b.inside or b.val() >= 2:
                        pe.wait_ge(res_ready, b.count(-2))
                    for t in range(T):
                        dst = psO[:, p, t * C:(t + 1) * C]
                        pe.matmul(dst, qT[:, p, t * P:(t + 1) * P],
                                  M_all[:, bass.ds(b.val(), 1), :].rearrange("p o c -> p (o c)"),
                                  start=True, stop=False)
                        for k in range(HC):
                            last = pe.matmul(dst, prT[:, p, k * N + t * P:k * N + (t + 1) * P], vw[:, p, k, :],
                                             start=False, stop=(k == HC - 1))
                    last.then_inc(out_done, 1)
                b = i.at(-1)
                if b.ok(NB):
                    p = b.par
                    pe.wait_ge(p3_ready, b.count())
                    if b.inside or b.val() >= 1:
                        pe.wait_ge(p3T_ready, b.count(-1))
                    for k in range(HC):
                        for t in range(T):
                            last = pe.transpose(psT[:, k * N + t * P:k * N + (t + 1) * P],
                                                pr[:, p, t * HS + k * P:t * HS + (k + 1) * P], ident[:, :])
                    last.then_inc(p3T_done, 1)

            run_steps(pe, step3, 0, LAST3, LO3, HI3)


def kernel(**inputs):
    import numpy as _np
    import concourse.bacc as _bacc
    from concourse import mybir as _mybir
    from concourse.bass_utils import run_bass_kernel_spmd as _run

    nc = _bacc.Bacc("TRN2", target_bir_lowering=False, num_devices=1)
    arrays, aps = {}, {}
    for name, value in inputs.items():
        v = _np.ascontiguousarray(value)
        arrays[f"in_{name}"] = v
        aps[name] = nc.dram_tensor(f"in_{name}", v.shape, _mybir.dt.from_np(v.dtype), kind="ExternalInput").ap()
    shape = inputs["L0_attn_x"].shape
    out = nc.dram_tensor("out", shape, _mybir.dt.float32, kind="ExternalOutput").ap()
    linear_attention_slot_experts_kernel(nc, aps, out)
    r = _run(nc, [arrays], core_ids=[0])
    return r.results[0]["out"]
```
